# Optimizing a Trainium2 kernel written in Bass

```python
import numpy as np
import jax
import jax.numpy as jnp

def _softmax(x, axis=-1):
    return jax.nn.softmax(x, axis=axis)
def _gelu(x):
    return jax.nn.gelu(x, approximate=True)
def _silu(x):
    return jax.nn.silu(x)
def _sigmoid(x):
    return jax.nn.sigmoid(x)
def _layernorm(x, axis=-1, eps=1e-5):
    m = jnp.mean(x, axis=axis, keepdims=True)
    v = jnp.var(x, axis=axis, keepdims=True)
    return (x - m) / jnp.sqrt(v + eps)
def _scatter_add(tgt, idx, src, axis=0):
    return tgt.at[idx].add(src)
def _segment_sum(src, seg, n):
    return jax.ops.segment_sum(src, seg, n)

kernel_name = 'mk_adj_seq_d2_adj_512_8e23d1'

def setup_inputs(seed: int = 0):
    np.random.seed(seed)
    _w = jnp.asarray
    def _rec_inputs():
        import jax
        import jax.numpy as jnp
        _gk = jax.random.key(seed)
        x = -0.0005207 + 1.001 * jax.random.normal(jax.random.fold_in(_gk, 1), (128, 128, 512), jnp.float32)
        _w = (1.0 + jnp.arange(128, dtype=jnp.float32)) ** -0.5
        _w = _w / _w.mean()
        _pij = jnp.clip(0.125 * _w[:, None] * _w[None, :], 0.0, 1.0)
        _a = jax.random.uniform(jax.random.fold_in(_gk, 2), (128, 128, 128)) < _pij
        _a = jnp.logical_or(_a, jnp.swapaxes(_a, -1, -2))
        _a = jnp.logical_or(_a, jnp.eye(128, dtype=bool))
        _af = _a.astype(jnp.float32)
        _af = _af * jax.random.uniform(jax.random.fold_in(_gk, 3), (128, 128, 128), jnp.float32, 0.05, 1)
        adj = _af
        return x, adj
    x, adj = _rec_inputs()
    def _L0_gnn_setup():
        import jax, jax.numpy as jnp
        import numpy as np
        NUM_HEADS = 8
        EPS = 1e-09
        key = jax.random.key(seed)
        ks = jax.random.split(key, 8)
        B, N, D = (2, 2048, 512)
        s = 1.0 / np.sqrt(D)
        x = jax.random.normal(ks[0], (B, N, D), dtype=jnp.float32)
        adjacency = jax.random.uniform(ks[1], (B, N, N), dtype=jnp.float32)
        W_q = jax.random.normal(ks[2], (D, D), dtype=jnp.float32) * s
        W_k = jax.random.normal(ks[3], (D, D), dtype=jnp.float32) * s
        W_v = jax.random.normal(ks[4], (D, D), dtype=jnp.float32) * s
        b_q = jnp.zeros((D,), jnp.float32)
        b_k = jnp.zeros((D,), jnp.float32)
        b_v = jnp.zeros((D,), jnp.float32)
        w_g = jax.random.normal(ks[5], (2 * D,), dtype=jnp.float32) * (1.0 / np.sqrt(2 * D))
        b_g = jnp.zeros((), jnp.float32)
        return {'x': x, 'adjacency': adjacency, 'W_q': W_q, 'b_q': b_q, 'W_k': W_k, 'b_k': b_k, 'W_v': W_v, 'b_v': b_v, 'w_g': w_g, 'b_g': b_g}
    _L0_gnn_all = _L0_gnn_setup()
    _L0_gnn_in = {k: v for k, v in _L0_gnn_all.items() if k in ('W_q', 'b_q', 'W_k', 'b_k', 'W_v', 'b_v', 'w_g', 'b_g', )}
    del _L0_gnn_all

    def _L1_gnn_setup():
        import jax, jax.numpy as jnp
        import numpy as np
        import math
        EMBED = 512
        DFF = 512
        B, N = (8, 2048)
        key = jax.random.key(seed)
        ks = jax.random.split(key, 8)
        node_fts = jax.random.normal(ks[0], (B, N, EMBED), dtype=jnp.float32)
        rel_edges = jax.random.randint(ks[1], (B, N, N), 0, 2).astype(jnp.float32)
        s = 1.0 / math.sqrt(EMBED)
        Wq = jax.random.normal(ks[2], (EMBED, DFF), dtype=jnp.float32) * s
        bq = jnp.zeros((DFF,), dtype=jnp.float32)
        Wk = jax.random.normal(ks[3], (EMBED, DFF), dtype=jnp.float32) * s
        bk = jnp.zeros((DFF,), dtype=jnp.float32)
        Wc = jax.random.normal(ks[4], (EMBED, EMBED), dtype=jnp.float32) * s
        gamma = jnp.ones((EMBED,), dtype=jnp.float32)
        beta = jnp.zeros((EMBED,), dtype=jnp.float32)
        return {'node_fts': node_fts, 'rel_edges': rel_edges, 'Wq': Wq, 'bq': bq, 'Wk': Wk, 'bk': bk, 'Wc': Wc, 'gamma': gamma, 'beta': beta}
    _L1_gnn_all = _L1_gnn_setup()
    _L1_gnn_in = {k: v for k, v in _L1_gnn_all.items() if k in ('Wq', 'bq', 'Wk', 'bk', 'Wc', 'gamma', 'beta', )}
    del _L1_gnn_all

    return {
        "x": x,
        "adj": adj,
        "L0_gnn_W_q": _L0_gnn_in["W_q"],
        "L0_gnn_b_q": _L0_gnn_in["b_q"],
        "L0_gnn_W_k": _L0_gnn_in["W_k"],
        "L0_gnn_b_k": _L0_gnn_in["b_k"],
        "L0_gnn_W_v": _L0_gnn_in["W_v"],
        "L0_gnn_b_v": _L0_gnn_in["b_v"],
        "L0_gnn_w_g": _L0_gnn_in["w_g"],
        "L0_gnn_b_g": _L0_gnn_in["b_g"],
        "L1_gnn_Wq": _L1_gnn_in["Wq"],
        "L1_gnn_bq": _L1_gnn_in["bq"],
        "L1_gnn_Wk": _L1_gnn_in["Wk"],
        "L1_gnn_bk": _L1_gnn_in["bk"],
        "L1_gnn_Wc": _L1_gnn_in["Wc"],
        "L1_gnn_gamma": _L1_gnn_in["gamma"],
        "L1_gnn_beta": _L1_gnn_in["beta"],
    }

def reference(x, adj, L0_gnn_W_q, L0_gnn_b_q, L0_gnn_W_k, L0_gnn_b_k, L0_gnn_W_v, L0_gnn_b_v, L0_gnn_w_g, L0_gnn_b_g, L1_gnn_Wq, L1_gnn_bq, L1_gnn_Wk, L1_gnn_bk, L1_gnn_Wc, L1_gnn_gamma, L1_gnn_beta):
    import jax
    import jax.numpy as jnp
    def _L0_gnn_ref(x, adjacency, W_q, b_q, W_k, b_k, W_v, b_v, w_g, b_g):
        import jax, jax.numpy as jnp
        import numpy as np
        NUM_HEADS = 8
        EPS = 1e-09
        B, N, D = x.shape
        H = NUM_HEADS
        hd = D // H
        Q = (x @ W_q + b_q).reshape(B, N, H, hd)
        K = (x @ W_k + b_k).reshape(B, N, H, hd)
        V = (x @ W_v + b_v).reshape(B, N, H, hd)
        scores = jnp.einsum('bihd,bjhd->bhij', Q, K) / jnp.sqrt(jnp.float32(hd))
        a = x @ w_g[:D]
        c = x @ w_g[D:]
        soul_bias = a[:, :, None] + c[:, None, :] + b_g
        scores = scores + (soul_bias + jnp.log(adjacency + EPS))[:, None, :, :]
        attn = jax.nn.softmax(scores, axis=-1)
        out = jnp.einsum('bhij,bjhd->bihd', attn, V).reshape(B, N, D)
        return out + x

    def _L1_gnn_ref(node_fts, rel_edges, Wq, bq, Wk, bk, Wc, gamma, beta):
        import jax, jax.numpy as jnp
        import numpy as np
        import math
        EMBED = 512
        DFF = 512
        B, N = (8, 2048)
        denom = math.sqrt(DFF)
        q = node_fts @ Wq + bq
        k = node_fts @ Wk + bk
        scores = jnp.einsum('bod,bid->boi', q, k) / denom
        mask = rel_edges == 0
        scores = jnp.where(mask, -1e+18, scores)
        attn = jax.nn.softmax(scores, axis=2)
        attn = jnp.where(mask, 0.0, attn)
        ctx = jnp.einsum('boi,bie->boe', attn, node_fts) @ Wc
        x = node_fts + ctx
        mu = jnp.mean(x, axis=-1, keepdims=True)
        var = jnp.mean(jnp.square(x - mu), axis=-1, keepdims=True)
        out = (x - mu) * jax.lax.rsqrt(var + 1e-05) * gamma + beta
        return out

    x = _L0_gnn_ref(x, adj, L0_gnn_W_q, L0_gnn_b_q, L0_gnn_W_k, L0_gnn_b_k, L0_gnn_W_v, L0_gnn_b_v, L0_gnn_w_g, L0_gnn_b_g)
    x = _L1_gnn_ref(x, adj, L1_gnn_Wq, L1_gnn_bq, L1_gnn_Wk, L1_gnn_bk, L1_gnn_Wc, L1_gnn_gamma, L1_gnn_beta)
    return x


_drawn_inputs = setup_inputs


def setup_inputs(seed=0):
    import zlib

    import numpy as np

    out = dict(_drawn_inputs(seed))
    spreads = {'L0_gnn_b_q': (0.0, 0.274),
     'L0_gnn_b_k': (0.0, 0.8),
     'L0_gnn_b_v': (0.0, 0.1),
     'L1_gnn_bq': (0.0, 0.305),
     'L1_gnn_bk': (0.0, 0.8),
     'L1_gnn_gamma': (1.0, 0.2),
     'L1_gnn_beta': (0.0, 0.1)}
    factors = {}
    for name, (base, spread) in spreads.items():
        noise = np.random.default_rng([zlib.crc32(name.encode()), seed]).standard_normal(out[name].shape)
        drawn = base * np.exp(spread * noise) if base else spread * noise
        out[name] = jnp.asarray(drawn.astype(out[name].dtype))
    for name, factor in factors.items():
        out[name] = (out[name] * factor).astype(out[name].dtype)
    return out
```

```python
from collections import namedtuple
from contextlib import ExitStack

import concourse.bass as bass
from concourse import mybir

P = 128
GRAPHS = 128
D = 512
HEADS = 8
HD = D // HEADS
C = D // P
GG = 4
NG = GRAPHS // GG
COLS = GG * P
PAIR = 2 * GG
HALF = PAIR // 2
EPS_ADJ = 1e-9
EPS_LN = 1e-5
MASKED = 1e18
SCALE0 = float(HD) ** -0.5
SCALE1 = float(D) ** -0.5
BIG = 3.0e38


Iteration = namedtuple("Iteration", "t u p par l0 l1 second nxt")


def gnn_program(nc, xT, x, adj, wq, wk, wv, wqT1, wkT1, wc, bq0, bk0, bv0, wg, bg, bq1, bk1,
                gamma, beta, ident_in, out):
    f32 = mybir.dt.float32
    f32r = mybir.dt.float32r
    bf16 = mybir.dt.bfloat16
    ALU = mybir.AluOpType
    ACT = mybir.ActivationFunctionType
    AX = mybir.AxisListType

    adj_v = adj.rearrange("g i j -> i g j")

    with ExitStack() as ctx:
        def sb(name, shape, dt=f32):
            return ctx.enter_context(nc.sbuf_tensor(name, shape, dt))

        def sem(name):
            return ctx.enter_context(nc.semaphore(name))

        w_hi = {n: sb(f"w{n}_hi", [P, C, D], f32r) for n in "qkvmc"}
        w_lo = {n: sb(f"w{n}_lo", [P, C, D], f32r) for n in "qkvmc"}
        xT_land = [sb(f"xT_land{i}", [P, C, COLS]) for i in range(2)]
        x_hi = sb("x_hi", [P, C, COLS], f32r)
        x_lo = sb("x_lo", [P, C, COLS], f32r)
        q_hi = sb("q_hi", [P, COLS], f32r)
        q_lo = sb("q_lo", [P, COLS], f32r)
        k_hi = sb("k_hi", [P, GG, 2 * P], f32r)
        k_lo = sb("k_lo", [P, GG, 2 * P], f32r)
        v_sb = sb("v_sb", [P, GG, D])
        probs = sb("probs", [P, PAIR, P])
        probsT = [sb(f"probsT{i}", [P, PAIR, P]) for i in range(2)]
        x1T = sb("x1T", [P, C, COLS])
        x1_hi = sb("x1_hi", [P, C, COLS], f32r)
        x1_lo = sb("x1_lo", [P, C, COLS], f32r)
        g_sb = [sb(f"g_sb{i}", [P, COLS]) for i in range(2)]
        y_hi = [sb(f"y_hi{i}", [P, D], f32r) for i in range(2)]
        y_lo = [sb(f"y_lo{i}", [P, D], f32r) for i in range(2)]
        x1n = sb("x1n", [P, GG, D])
        xn = [sb(f"xn{i}", [P, D]) for i in range(2)]
        adj_sb = [sb(f"adj_sb{i}", [P, GG, P]) for i in range(2)]
        ln_adj = sb("ln_adj", [P, GG, P])
        bias0 = sb("bias0", [P, GG, P])
        mask = sb("mask", [P, GG, P], bf16)
        att1 = sb("att1", [P, GG, P])
        att1T_hi = sb("att1T_hi", [P, GG, P], f32r)
        att1T_lo = sb("att1T_lo", [P, GG, P], f32r)
        scratch = sb("scratch", [P, D])
        bv_b = sb("bv_b", [P, D])
        gamma_b = sb("gamma_b", [P, D])
        beta_b = sb("beta_b", [P, D])
        wg1_b = sb("wg1_b", [P, D])
        wg2_b = sb("wg2_b", [P, D])
        v1_b = sb("v1_b", [P, D])
        ident = sb("ident", [P, P])
        cols = sb("cols", [P, 4 * C])
        bq0_c, bk0_c, bq1_c, bk1_c = (cols[:, C * i:C * (i + 1)] for i in range(4))
        consts = sb("consts", [P, 16])
        bg_c, nbg_c, r0_c, half_c, eps_c, eps1_c, minus_c = (consts[:, i:i + 1] for i in range(7))
        u1_c = consts[:, 8:8 + C]
        nbq0_c = consts[:, 12:12 + C]
        carrier = sb("carrier", [P, 2 * C + GG])
        a_c = sb("a_c", [P, GG])
        c_c = sb("c_c", [P, GG])
        r_c = sb("r_c", [P, GG])
        nmax = sb("nmax", [P, PAIR])
        sums = sb("sums", [P, PAIR])
        rcp = sb("rcp", [P, PAIR])
        stats1 = sb("stats1", [P, 3 * GG])
        nmax1, sums1, rcp1 = (stats1[:, GG * i:GG * (i + 1)] for i in range(3))
        bnst = sb("bnst", [P, 6])
        lnst = sb("lnst", [P, GG, 4])

        bank = [ctx.enter_context(nc.psum_tensor(f"bank{i}", [P, 512], f32)) for i in range(8)]

        PER = dict(pe_qk=8, pe_cb=1, pe_s=8, pe_t=8, pe_v=4, pe_pv=4, pe_g=4, pe_x=4, pe_sa=1,
                   pe_y=4, pe_tp=1, pe_ctx=4,
                   act_q=4, act_k=4, act_exp=2 * C, act_pt=2 * C, act_x1=4, act_g=4, act_x1n=4,
                   act_y=4, act_ln=1, act_exp1=1, act_tp=1, act_nrm=4,
                   dve_q=4, dve_k=4, dve_b=1, dve_max=2 * C, dve_rcp=2 * C, dve_v=4, dve_pv=4,
                   dve_x1=4, dve_a=4, dve_r=4, dve_mask=1, dve_sa=1, dve_sub=1, dve_max1=1,
                   dve_rcp1=1, dve_att1=1, dve_tp=1, dve_y=4, dve_res=4, dve_bn=4, dve_mean=4,
                   dve_x=4, act_x=4, pool_p=2 * C, pool_eps=4, pool_rstd=4, pool_nmr=4,
                   pool_gam=4, pool_out=4)
        s = {n: sem(n) for n in PER}
        s_xT = [sem(f"xT_loaded{i}") for i in range(2)]
        s_adj = [sem(f"adj_loaded{i}") for i in range(2)]
        s_xn = [sem(f"xn_loaded{i}") for i in range(2)]
        s_out = [sem(f"out_stored{i}") for i in range(GG)]
        s_wld = {n: sem(f"w{n}_loaded") for n in ("q", "k", "v", "q1", "k1", "c")}
        s_const = sem("const_loaded")
        s_zero = sem("pool_zeroed")
        s_whi = sem("act_w_hi")
        s_wlo = sem("dve_w_lo")
        s_m = sem("pe_m")
        s_cst = sem("dve_const")
        s_half = sem("dve_half")

        def nth(name, t, k=0):
            return t * PER[name] + k + 1

        def hi_lo(out_ap, st, mv):
            n = len(st)
            for i in range(n):
                (sh, sl), (mh, ml) = st[i], mv[i]
                nc.tensor.matmul(out_ap, sh, mh, start=(i == 0), stop=False)
                nc.tensor.matmul(out_ap, sh, ml, start=False, stop=False)
                last = nc.tensor.matmul(out_ap, sl, mh, start=False, stop=(i == n - 1))
            return last

        def w_cols(n, c):
            return [(w_hi[n][:, d, c * P:(c + 1) * P], w_lo[n][:, d, c * P:(c + 1) * P]) for d in range(C)]

        def w_rows(n):
            return [(w_hi[n][:, d, :], w_lo[n][:, d, :]) for d in range(C)]

        def act_cols(hi, lo):
            return [(hi[:, d, :], lo[:, d, :]) for d in range(C)]

        def act_rows(hi, lo, g):
            return [(hi[:, d, g * P:(g + 1) * P], lo[:, d, g * P:(g + 1) * P]) for d in range(C)]

        def flat(t):
            return t[:, :, :].rearrange("p a b -> p (a b)")


        def iterations(eng, body):
            def step(p, par, **kinds):
                t = 2 * p + par
                body(Iteration(**{**dict(t=t, u=t - 1, p=p, par=par, l0=True, l1=True, second=False,
                                         nxt=True), **kinds}))
            step(0, 0, l1=False)
            step(0, 1, second=True)
            with eng.Fori(1, NG // 2 - 1) as p:
                step(p, 0)
                step(p, 1)
            step(NG // 2 - 1, 0)
            step(NG // 2 - 1, 1, nxt=False)
            step(NG // 2, 0, l0=False, nxt=False)

        block = ctx.enter_context(nc.Block())

        @block.sync
        def _(sp):
            def load_xT(t, par):
                sp.dma_start(flat(xT_land[par]), xT[bass.ds(t * P, P), :]).then_inc(s_xT[par], 16)

            def load_adj(t, par):
                sp.dma_start(adj_sb[par][:, :, :], adj_v[:, bass.ds(t * GG, GG), :]).then_inc(s_adj[par], 16)

            def load_xn(t, g):
                sp.dma_start(xn[g % 2][:, :], x[bass.ds(t * COLS + g * P, P), :]).then_inc(s_xn[g % 2], 16)

            sp.dma_start(ident[:, :], ident_in).then_inc(s_const, 16)
            sp.dma_start(bq1_c, bq1).then_inc(s_const, 16)
            sp.dma_start(bk1_c, bk1).then_inc(s_const, 16)
            sp.dma_start(x1T[:, :, :], wqT1).then_inc(s_wld["q1"], 16)
            sp.dma_start(x1n[:, :, :], wkT1).then_inc(s_wld["k1"], 16)
            sp.dma_start(xT_land[1][:, :, :], wq).then_inc(s_wld["q"], 16)
            sp.dma_start(v_sb[:, :, :], wk).then_inc(s_wld["k"], 16)
            load_xT(0, 0)
            for i in range(2):
                sp.dma_start(flat(probsT[i]), wv[:, 2 * i:2 * i + 2, :].rearrange("p a b -> p (a b)"))\
                  .then_inc(s_wld["v"], 16)
            sp.dma_start(bq0_c, bq0).then_inc(s_const, 16)
            sp.dma_start(bk0_c, bk0).then_inc(s_const, 16)
            sp.dma_start(bg_c, bg.to_broadcast([P, 1])).then_inc(s_const, 16)
            sp.dma_start(wg1_b[:, :], wg[:, 0:D].to_broadcast([P, D])).then_inc(s_const, 16)
            sp.dma_start(wg2_b[:, :], wg[:, D:2 * D].to_broadcast([P, D])).then_inc(s_const, 16)
            sp.dma_start(bv_b[:, :], bv0.to_broadcast([P, D])).then_inc(s_const, 16)
            sp.dma_start(gamma_b[:, :], gamma.to_broadcast([P, D])).then_inc(s_const, 16)
            sp.dma_start(beta_b[:, :], beta.to_broadcast([P, D])).then_inc(s_const, 16)
            load_adj(0, 0)
            load_xn(0, 0)
            load_xn(0, 1)
            sp.wait_ge(s["dve_a"], nth("dve_a", 0, 0))
            load_xn(0, 2)
            sp.wait_ge(s["dve_a"], nth("dve_a", 0, 1))
            load_xn(0, 3)
            sp.wait_ge(s_m, 1)
            sp.dma_start(x1T[:, :, :], wc).then_inc(s_wld["c"], 16)

            def body(it):
                t, u = it.t, it.u
                if it.nxt:
                    if it.l1:
                        sp.wait_ge(s["dve_pv"], nth("dve_pv", u, 3))
                    else:
                        sp.wait_ge(s_wlo, 1)
                    load_xT(t + 1, 1 - it.par)
                    for g in range(2):
                        sp.wait_ge(s["dve_a"], nth("dve_a", t, g + 2))
                        load_xn(t + 1, g)
                    if it.l1:
                        sp.wait_ge(s["dve_mask"], nth("dve_mask", u))
                    load_adj(t + 1, 1 - it.par)

                def store(g):
                    sp.wait_ge(s["pool_out"], nth("pool_out", u, g))
                    sp.dma_start(out[bass.ds(u * COLS + g * P, P), :], x1n[:, g, :]).then_inc(s_out[g], 16)

                if it.l1:
                    store(0)
                    store(1)
                if it.nxt:
                    for g in range(2, 4):
                        sp.wait_ge(s["dve_a"], nth("dve_a", t + 1, g - 2))
                        load_xn(t + 1, g)
                if it.l1:
                    store(2)
                    store(3)

            iterations(sp, body)
            for g in range(GG):
                sp.wait_ge(s_out[g], 16 * NG)

        @block.tensor
        def _(pe):
            pe.wait_ge(s_wld["q1"], 16)
            pe.wait_ge(s_wld["k1"], 16)
            pe.wait_ge(s_const, 16 * 11)
            for d in range(C):
                for f in range(C):
                    mm = nc.tensor.matmul(bank[d][:, :], x1T[:, f, d * P:(d + 1) * P], x1n[:, f, :],
                                          start=(f == 0), stop=(f == C - 1))
            for f in range(C):
                mm = nc.tensor.matmul(bank[4][:, :], bk1_c[:, f:f + 1].to_broadcast([P, P]), x1T[:, f, :],
                                      start=(f == 0), stop=(f == C - 1))
            for f in range(C):
                mm = nc.tensor.matmul(bank[5][:, 0:1], bk1_c[:, f:f + 1].to_broadcast([P, P]),
                                      bq1_c[:, f:f + 1], start=(f == 0), stop=(f == C - 1))
            for d in range(C):
                for f in range(C):
                    mm = nc.tensor.matmul(bank[5][:, 1 + d:2 + d], x1n[:, f, d * P:(d + 1) * P],
                                          bq1_c[:, f:f + 1], start=(f == 0), stop=(f == C - 1))
            mm.then_inc(s_m, 1)

            def qk(t, c, first):
                if c == 0:
                    if first:
                        pe.wait_ge(s_wlo, 7)
                        pe.wait_ge(s["dve_x"], nth("dve_x", t, C - 1))
                    else:
                        pe.wait_ge(s["dve_x"], nth("dve_x", t, C - 1))
                        pe.wait_ge(s["dve_q"], nth("dve_q", t - 1, 3))
                hi_lo(bank[0][:, :], w_cols("q", c), act_cols(x_hi, x_lo)).then_inc(s["pe_qk"], 1)
                hi_lo(bank[1][:, :], w_cols("k", c), act_cols(x_hi, x_lo)).then_inc(s["pe_qk"], 1)

            def v(t, g, first, second):
                if g < 2 and not first and not second:
                    pe.wait_ge(s["dve_res"], nth("dve_res", t - 2, g + 2))
                if g < 2 and second:
                    pe.wait_ge(s["dve_v"], nth("dve_v", t - 1, g + 2))
                if g >= 2:
                    pe.wait_ge(s["dve_v"], nth("dve_v", t, g - 2))
                hi_lo(bank[2 + g % 2][:, :], act_rows(x_hi, x_lo, g), w_rows("v")).then_inc(s["pe_v"], 1)

            def scores(t, c):
                pe.wait_ge(s["dve_q"], nth("dve_q", t, c))
                pe.wait_ge(s["dve_k"], nth("dve_k", t, c))
                for g in range(GG):
                    if g == 0 and c > 0:
                        pe.wait_ge(s["dve_max"], nth("dve_max", t, 2 * c - 2))
                    if g == 2 and c > 0:
                        pe.wait_ge(s["dve_max"], nth("dve_max", t, 2 * c - 1))
                    if g == 2 and c == 0:
                        pe.wait_ge(s["dve_b"], nth("dve_b", t))
                    cols_g = slice(g * P, (g + 1) * P)
                    mm = hi_lo(bank[4 + g // 2][:, (g % 2) * 2 * P:(g % 2 + 1) * 2 * P],
                               [(q_hi[:, cols_g], q_lo[:, cols_g])], [(k_hi[:, g, :], k_lo[:, g, :])])
                    if g % 2:
                        mm.then_inc(s["pe_s"], 1)

            def turn(t, c):
                for h in range(2):
                    pe.wait_ge(s["pool_p"], nth("pool_p", t, 2 * c + h))
                    for k in range(HALF):
                        mm = nc.tensor.transpose(bank[6 + h][:, k * P:(k + 1) * P],
                                                 probs[:, h * HALF + k, :], ident[:, :])
                    mm.then_inc(s["pe_t"], 1)

            def pv(t, c, b):
                for h in range(2):
                    pe.wait_ge(s["act_pt"], nth("act_pt", t, 2 * c + h))
                    if c == 0 and h == 0:
                        pe.wait_ge(s["dve_v"], nth("dve_v", t, GG - 1))
                    for g in range(2 * h, 2 * h + 2):
                        for e in range(2):
                            mm = nc.tensor.matmul(bank[b][e * HD:(e + 1) * HD, g * P:(g + 1) * P],
                                                  v_sb[:, g, c * P + e * HD:c * P + (e + 1) * HD],
                                                  probsT[c % 2][:, 2 * g + e, :], start=True, stop=True)
                mm.then_inc(s["pe_pv"], 1)

            def body(it):
                t, u = it.t, it.u
                first, second, last = not it.l1, it.second, not it.l0
                if not last:
                    qk(t, 0, first)
                    if not first:
                        pe.wait_ge(s["dve_max"], nth("dve_max", t - 1, 2 * C - 1))
                    else:
                        pe.wait_ge(s["dve_a"], nth("dve_a", t, 3))
                        pe.wait_ge(s_cst, 1)
                    if not first:
                        pe.wait_ge(s["dve_a"], nth("dve_a", t, 3))
                    for g in range(GG):
                        mm = nc.tensor.transpose(bank[5][:, g * P:(g + 1) * P],
                                                 c_c[:, g:g + 1].to_broadcast([P, P]), ident[:, :])
                    mm.then_inc(s["pe_cb"], 1)
                    v(t, 0, first, second)
                if not first:
                    pe.wait_ge(s["dve_pv"], nth("dve_pv", u, 2))
                    pe.wait_ge(s["act_pt"], nth("act_pt", u, 5))
                    turn(u, 3)
                if not last:
                    v(t, 1, first, second)
                if not first:
                    pv(u, 3, 6)
                if not last:
                    scores(t, 0)
                    v(t, 2, first, second)
                    v(t, 3, first, second)
                    pe.wait_ge(s["dve_q"], nth("dve_q", t, 0))
                    pe.wait_ge(s["dve_k"], nth("dve_k", t, 0))
                    qk(t, 1, first)

                def gw(c):
                    if c < 2:
                        if not last:
                            pe.wait_ge(s["dve_v"], nth("dve_v", t, c + 2))
                        else:
                            pe.wait_ge(s["dve_res"], nth("dve_res", u - 1, c + 2))
                        if c == 0:
                            pe.wait_ge(s["dve_x1"], nth("dve_x1", u, 3))
                            if second:
                                pe.wait_ge(s_wlo, 8)
                    else:
                        pe.wait_ge(s["act_g"], nth("act_g", u, c - 2))
                    hi_lo(bank[2 + c % 2][:, :], w_cols("m", c), act_cols(x1_hi, x1_lo)).then_inc(s["pe_g"], 1)

                def xw(g):
                    if g == 0:
                        if not last:
                            pe.wait_ge(s["dve_k"], nth("dve_k", t, 1))
                        else:
                            pe.wait_ge(s["dve_k"], nth("dve_k", u, 3))
                    else:
                        pe.wait_ge(s["act_x1n"], nth("act_x1n", u, g - 1))
                    for d in range(C):
                        mm = nc.tensor.transpose(bank[1][:, d * P:(d + 1) * P],
                                                 x1T[:, d, g * P:(g + 1) * P], ident[:, :])
                    mm.then_inc(s["pe_x"], 1)

                def sa(c):
                    if c == 0:
                        if not last:
                            pe.wait_ge(s["dve_q"], nth("dve_q", t, 1))
                        else:
                            pe.wait_ge(s["dve_q"], nth("dve_q", u, 3))
                    pe.wait_ge(s["act_g"], nth("act_g", u, c))
                    for g in range(GG):
                        cols_g = slice(g * P, (g + 1) * P)
                        mm = nc.tensor.matmul(bank[0][:, cols_g], g_sb[c % 2][:, cols_g], x1T[:, c, cols_g],
                                              start=(c == 0 and g == 0), stop=(c == C - 1),
                                              skip_group_check=True)
                    if c == C - 1:
                        mm.then_inc(s["pe_sa"], 1)

                def yw(g):
                    if g < 2:
                        pe.wait_ge(s["act_g"], nth("act_g", u, g + 2))
                    else:
                        pe.wait_ge(s["dve_y"], nth("dve_y", u, g - 2))
                    hi_lo(bank[2 + g % 2][:, :], act_rows(x1_hi, x1_lo, g), w_rows("c")).then_inc(s["pe_y"], 1)

                def cx(g, b):
                    pe.wait_ge(s["dve_y"], nth("dve_y", u, g))
                    hi_lo(bank[b][:, :], [(att1T_hi[:, g, :], att1T_lo[:, g, :])],
                          [(y_hi[g % 2][:, :], y_lo[g % 2][:, :])]).then_inc(s["pe_ctx"], 1)

                if not first:
                    gw(0)
                    xw(0)
                    gw(1)
                    xw(1)
                if not last:
                    if not first:
                        pe.wait_ge(s["dve_pv"], nth("dve_pv", u, 3))
                        pe.wait_ge(s["act_pt"], nth("act_pt", u, 7))
                    turn(t, 0)
                if not first:
                    sa(0)
                    gw(2)
                    xw(2)
                    sa(1)
                    gw(3)
                    xw(3)
                    sa(2)
                if not last:
                    scores(t, 1)
                if not first:
                    sa(3)
                    yw(0)
                    yw(1)
                if not last:
                    if first:
                        pe.wait_ge(s["dve_q"], nth("dve_q", t, 1))
                    else:
                        pe.wait_ge(s["dve_sa"], nth("dve_sa", u))
                        pe.wait_ge(s["act_x1n"], nth("act_x1n", u, 3))
                    pe.wait_ge(s["dve_k"], nth("dve_k", t, 1))
                    qk(t, 2, first)
                if not first:
                    if not last:
                        pe.wait_ge(s["dve_max"], nth("dve_max", t, 3))
                    else:
                        pe.wait_ge(s["dve_max"], nth("dve_max", u, 7))
                    pe.wait_ge(s["dve_att1"], nth("dve_att1", u))
                    for g in range(GG):
                        mm = nc.tensor.transpose(bank[5][:, g * P:(g + 1) * P], att1[:, g, :], ident[:, :])
                    mm.then_inc(s["pe_tp"], 1)
                if not last:
                    pe.wait_ge(s["act_pt"], nth("act_pt", t, 1))
                    turn(t, 1)
                if not first:
                    pe.wait_ge(s["dve_tp"], nth("dve_tp", u))
                    if not last:
                        pe.wait_ge(s["dve_q"], nth("dve_q", t, 2))
                    else:
                        pe.wait_ge(s["dve_sa"], nth("dve_sa", u))
                    cx(0, 0)
                    if not last:
                        pe.wait_ge(s["dve_k"], nth("dve_k", t, 2))
                    else:
                        pe.wait_ge(s["act_x1n"], nth("act_x1n", u, 3))
                    cx(1, 1)
                    yw(2)
                    yw(3)
                if not last:
                    pe.wait_ge(s["act_pt"], nth("act_pt", t, 2))
                    pv(t, 0, 6)
                    if not first:
                        pe.wait_ge(s["dve_tp"], nth("dve_tp", u))
                    scores(t, 2)
                    pe.wait_ge(s["act_pt"], nth("act_pt", t, 3))
                    pv(t, 1, 7)
                    pe.wait_ge(s["dve_q"], nth("dve_q", t, 2))
                    pe.wait_ge(s["dve_k"], nth("dve_k", t, 2))
                    if not first:
                        pe.wait_ge(s["dve_res"], nth("dve_res", u, 0))
                        pe.wait_ge(s["dve_res"], nth("dve_res", u, 1))
                    qk(t, 3, first)
                if not first:
                    cx(2, 2)
                if not last:
                    pe.wait_ge(s["dve_pv"], nth("dve_pv", t, 0))
                    pe.wait_ge(s["dve_pv"], nth("dve_pv", t, 1))
                    turn(t, 2)
                if not first:
                    cx(3, 3)
                if not last:
                    scores(t, 3)
                    pv(t, 2, 6)

            iterations(pe, body)

        @block.scalar
        def _(act):
            act.wait_ge(s_wld["q"], 16)
            nc.scalar.activation(w_hi["q"][:, :, :], xT_land[1][:, :, :], ACT.Copy, scale=-SCALE0)\
              .then_inc(s_whi, 1)
            act.wait_ge(s_wld["k"], 16)
            nc.scalar.activation(w_hi["k"][:, :, :], v_sb[:, :, :], ACT.Copy).then_inc(s_whi, 1)
            act.wait_ge(s_wld["v"], 32)
            for i in range(2):
                op = nc.scalar.activation(w_hi["v"][:, 2 * i:2 * i + 2, :].rearrange("p a b -> p (a b)"),
                                          flat(probsT[i]), ACT.Copy)
            op.then_inc(s_whi, 1)
            act.wait_ge(s_m, 1)
            for d in range(C):
                nc.scalar.activation(w_hi["m"][:, d, :], bank[d][:, :], ACT.Copy, scale=-SCALE1)\
                  .then_inc(s_whi, 1)
            act.wait_ge(s_cst, 1)
            act.wait_ge(s_zero, 1)

            def log_adj(t, loads, par):
                act.wait_ge(s_adj[par], 16 * loads)
                nc.scalar.activation(ln_adj[:, :, :], adj_sb[par][:, :, :], ACT.Ln,
                                     bias=eps_c).then_inc(s["act_ln"], 1)

            log_adj(0, 1, 0)

            def x_hi_part(t, loads, par):
                act.wait_ge(s_xT[par], 16 * loads)
                for c in range(C):
                    nc.scalar.activation(x_hi[:, c, :], xT_land[par][:, c, :], ACT.Copy)\
                      .then_inc(s["act_x"], 1)

            x_hi_part(0, 1, 0)

            def qk_hi(t, c):
                act.wait_ge(s["pe_qk"], nth("pe_qk", t, 2 * c))
                nc.scalar.activation(q_hi[:, :], bank[0][:, :], ACT.Identity,
                                     bias=nbq0_c[:, c:c + 1]).then_inc(s["act_q"], 1)
                act.wait_ge(s["pe_qk"], nth("pe_qk", t, 2 * c + 1))
                for e in range(2):
                    r = slice(e * HD, (e + 1) * HD)
                    op = nc.scalar.activation(k_hi[r, :, e * P:(e + 1) * P],
                                              bank[1][r, :].rearrange("p (g j) -> p g j", g=GG),
                                              ACT.Identity, bias=bk0_c[r, c:c + 1])
                op.then_inc(s["act_k"], 1)

            def exps(t, c):
                for h in range(2):
                    act.wait_ge(s["dve_max"], nth("dve_max", t, 2 * c + h))
                    for k in range(h * HALF, (h + 1) * HALF):
                        op = nc.scalar.activation(probs[:, k, :], probs[:, k, :], ACT.Exp,
                                                  bias=nmax[:, k:k + 1], scale=-1.0,
                                                  accum_out=sums[:, k:k + 1])
                    op.then_inc(s["act_exp"], 1)

            def turned(t, c):
                for h in range(2):
                    act.wait_ge(s["pe_t"], nth("pe_t", t, 2 * c + h))
                    nc.scalar.activation(probsT[c % 2][:, h * HALF:(h + 1) * HALF, :]
                                         .rearrange("p a b -> p (a b)"),
                                         bank[6 + h][:, :], ACT.Copy).then_inc(s["act_pt"], 1)

            def x1hi(t, c):
                act.wait_ge(s["dve_pv"], nth("dve_pv", t, c))
                nc.scalar.activation(x1_hi[:, c, :], x1T[:, c, :], ACT.Copy).then_inc(s["act_x1"], 1)

            def body(it):
                t, u = it.t, it.u

                def g_out(c):
                    act.wait_ge(s["pe_g"], nth("pe_g", u, c))
                    nc.scalar.activation(g_sb[c % 2][:, :], bank[2 + c % 2][:, :], ACT.Identity,
                                         bias=u1_c[:, c:c + 1]).then_inc(s["act_g"], 1)

                def x1_out(g):
                    act.wait_ge(s["pe_x"], nth("pe_x", u, g))
                    if not it.second:
                        act.wait_ge(s_out[g], 16 * u)
                    nc.scalar.activation(x1n[:, g, :], bank[1][:, :], ACT.Copy).then_inc(s["act_x1n"], 1)

                def y_out(g):
                    act.wait_ge(s["pe_y"], nth("pe_y", u, g))
                    nc.scalar.activation(y_hi[g % 2][:, :], bank[2 + g % 2][:, :], ACT.Copy)\
                      .then_inc(s["act_y"], 1)

                def norm(g):
                    act.wait_ge(s["pool_nmr"], nth("pool_nmr", u, g))
                    nc.scalar.activation(x1n[:, g, :], x1n[:, g, :], ACT.Identity,
                                         bias=lnst[:, g, 3:4], scale=lnst[:, g, 2:3]).then_inc(s["act_nrm"], 1)

                if it.l0:
                    qk_hi(t, 0)
                if it.l1:
                    turned(u, 3)
                    x1hi(u, 3)
                if it.l0:
                    exps(t, 0)
                    qk_hi(t, 1)
                if it.l1:
                    g_out(0)
                    x1_out(0)
                    g_out(1)
                    x1_out(1)
                if it.l0:
                    turned(t, 0)
                if it.l1:
                    g_out(2)
                    x1_out(2)
                    g_out(3)
                    x1_out(3)
                if it.l0:
                    exps(t, 1)
                if it.l1:
                    act.wait_ge(s["dve_max1"], nth("dve_max1", u))
                    for g in range(GG):
                        op = nc.scalar.activation(att1[:, g, :], att1[:, g, :], ACT.Exp,
                                                  bias=nmax1[:, g:g + 1], scale=-1.0,
                                                  accum_out=sums1[:, g:g + 1])
                    op.then_inc(s["act_exp1"], 1)
                    y_out(0)
                    y_out(1)
                if it.l0:
                    qk_hi(t, 2)
                if it.l1:
                    act.wait_ge(s["pe_tp"], nth("pe_tp", u))
                    nc.scalar.activation(flat(att1T_hi), bank[5][:, :], ACT.Copy).then_inc(s["act_tp"], 1)
                if it.l0:
                    turned(t, 1)
                if it.l1:
                    y_out(2)
                    norm(0)
                    y_out(3)
                    norm(1)
                if not it.l1:
                    act.wait_ge(s_wld["c"], 16)
                    nc.scalar.activation(w_hi["c"][:, :, :], x1T[:, :, :], ACT.Copy).then_inc(s_whi, 1)
                if it.l0:
                    x1hi(t, 0)
                    exps(t, 2)
                    x1hi(t, 1)
                    qk_hi(t, 3)
                if it.nxt:
                    act.wait_ge(s["pe_qk"], nth("pe_qk", t, 2 * C - 1))
                    x_hi_part(t + 1, it.p + 1 + it.par, 1 - it.par)
                if it.l1:
                    norm(2)
                if it.l0:
                    turned(t, 2)
                if it.l1:
                    norm(3)
                if it.nxt:
                    act.wait_ge(s["dve_b"], nth("dve_b", t))
                    log_adj(t + 1, it.p + 1 + it.par, 1 - it.par)
                if it.l0:
                    exps(t, 3)
                    x1hi(t, 2)

            iterations(act, body)

        @block.vector
        def _(dve):
            nc.vector.memset(eps_c, EPS_ADJ)
            nc.vector.memset(eps1_c, EPS_LN)
            nc.vector.memset(minus_c, -1.0)
            nc.vector.memset(half_c, -0.5).then_inc(s_half, 1)
            dve.wait_ge(s_const, 16 * 11)
            nc.vector.tensor_scalar(nbq0_c, bq0_c, -SCALE0, None, ALU.mult)
            nc.vector.tensor_scalar(nbg_c, bg_c, -1.0, None, ALU.mult)
            dve.wait_ge(s_whi, 1)
            nc.vector.scalar_tensor_tensor(out=flat(w_lo["q"]), in0=flat(xT_land[1]), scalar=-SCALE0,
                                           in1=flat(w_hi["q"]).bitcast(f32), op0=ALU.mult,
                                           op1=ALU.subtract).then_inc(s_wlo, 1)
            dve.wait_ge(s_whi, 2)
            nc.vector.tensor_tensor(flat(w_lo["k"]), flat(v_sb), flat(w_hi["k"]).bitcast(f32),
                                    ALU.subtract).then_inc(s_wlo, 1)
            dve.wait_ge(s_whi, 3)
            for i in range(2):
                half = slice(2 * i, 2 * i + 2)
                op = nc.vector.tensor_tensor(w_lo["v"][:, half, :].rearrange("p a b -> p (a b)"),
                                             flat(probsT[i]),
                                             w_hi["v"][:, half, :].rearrange("p a b -> p (a b)").bitcast(f32),
                                             ALU.subtract)
            op.then_inc(s_wlo, 1)
            for d in range(C):
                dve.wait_ge(s_whi, 4 + d)
                nc.vector.scalar_tensor_tensor(out=w_lo["m"][:, d, :], in0=bank[d][:, :], scalar=-SCALE1,
                                               in1=w_hi["m"][:, d, :].bitcast(f32), op0=ALU.mult,
                                               op1=ALU.subtract).then_inc(s_wlo, 1)
            nc.vector.tensor_scalar(v1_b[:, :], bank[4][:, :], -SCALE1, None, ALU.mult)
            nc.vector.tensor_scalar(r0_c, bank[5][:, 0:1], -SCALE1, None, ALU.mult)
            nc.vector.tensor_scalar(u1_c, bank[5][:, 1:1 + C], -SCALE1, None, ALU.mult).then_inc(s_cst, 1)
            dve.wait_ge(s_cst, 1)
            dve.wait_ge(s_zero, 1)

            def carry_wait(semaphore, value, word):
                dve.wait_ge(semaphore, value)
                nc.vector.memset(carrier[0:1, word:word + 1], 0.0)

            def qk_lo(t, c):
                dve.wait_ge(s["act_q"], nth("act_q", t, c))
                nc.vector.scalar_tensor_tensor(out=q_lo[:, :], in0=bank[0][:, :], scalar=nbq0_c[:, c:c + 1],
                                               in1=q_hi[:, :].bitcast(f32), op0=ALU.add,
                                               op1=ALU.subtract).then_inc(s["dve_q"], 1)
                dve.wait_ge(s["act_k"], nth("act_k", t, c))
                for e in range(2):
                    r = slice(e * HD, (e + 1) * HD)
                    op = nc.vector.scalar_tensor_tensor(
                        out=k_lo[r, :, e * P:(e + 1) * P],
                        in0=bank[1][r, :].rearrange("p (g j) -> p g j", g=GG), scalar=bk0_c[r, c:c + 1],
                        in1=k_hi[r, :, e * P:(e + 1) * P].bitcast(f32), op0=ALU.add, op1=ALU.subtract)
                op.then_inc(s["dve_k"], 1)

            def v_out(t, g):
                dve.wait_ge(s["pe_v"], nth("pe_v", t, g))
                nc.vector.tensor_tensor(v_sb[:, g, :], bank[2 + g % 2][:, :], bv_b[:, :], ALU.add)\
                  .then_inc(s["dve_v"], 1)

            def bias(t):
                dve.wait_ge(s["pe_cb"], nth("pe_cb", t))
                dve.wait_ge(s["act_ln"], nth("act_ln", t))
                for g in range(GG):
                    op = nc.vector.scalar_tensor_tensor(out=bias0[:, g, :], in0=bank[5][:, g * P:(g + 1) * P],
                                                        scalar=a_c[:, g:g + 1], in1=ln_adj[:, g, :],
                                                        op0=ALU.add, op1=ALU.subtract)
                op.then_inc(s["dve_b"], 1)

            def maxima(t, c):
                for h in range(2):
                    if c == 0 and h == 0:
                        dve.wait_ge(s["dve_b"], nth("dve_b", t))
                    carry_wait(s["pe_s"], nth("pe_s", t, 2 * c + h), 2 * c + h)
                    for k in range(h * HALF, (h + 1) * HALF):
                        op = nc.vector.tensor_tensor_reduce(
                            out=probs[:, k, :], in0=bank[4 + h][:, (k % HALF) * P:(k % HALF + 1) * P],
                            in1=bias0[:, k // 2, :], scale=1.0, scalar=BIG, op0=ALU.add, op1=ALU.min,
                            accum_out=nmax[:, k:k + 1])
                    op.then_inc(s["dve_max"], 1)

            def recips(t, c):
                for h in range(2):
                    dve.wait_ge(s["act_exp"], nth("act_exp", t, 2 * c + h))
                    half = slice(h * HALF, (h + 1) * HALF)
                    nc.vector.reciprocal(rcp[:, half], sums[:, half]).then_inc(s["dve_rcp"], 1)

            def residual0(t, c, b, par):
                dve.wait_ge(s["pe_pv"], nth("pe_pv", t, c))
                nc.vector.tensor_tensor(x1T[:, c, :], bank[b][:, :], xT_land[par][:, c, :], ALU.add)\
                  .then_inc(s["dve_pv"], 1)

            def x1lo(t, c):
                dve.wait_ge(s["act_x1"], nth("act_x1", t, c))
                nc.vector.tensor_tensor(x1_lo[:, c, :], x1T[:, c, :], x1_hi[:, c, :].bitcast(f32),
                                        ALU.subtract).then_inc(s["dve_x1"], 1)

            def x_lo_part(t, par):
                for c in range(C):
                    dve.wait_ge(s["act_x"], nth("act_x", t, c))
                    nc.vector.tensor_tensor(x_lo[:, c, :], xT_land[par][:, c, :],
                                            x_hi[:, c, :].bitcast(f32), ALU.subtract)\
                      .then_inc(s["dve_x"], 1)

            def gates(t, loads):
                for g in range(GG):
                    dve.wait_ge(s_xn[g % 2], 16 * (loads + g // 2))
                    if g > 0:
                        dve.wait_ge(s["dve_a"], nth("dve_a", t, g - 1))
                    nc.vector.tensor_tensor_reduce(out=scratch[:, :], in0=xn[g % 2][:, :], in1=wg1_b[:, :],
                                                   scale=-1.0, scalar=nbg_c, op0=ALU.mult, op1=ALU.add,
                                                   accum_out=a_c[:, g:g + 1])
                    nc.vector.tensor_tensor_reduce(out=xn[g % 2][:, :], in0=xn[g % 2][:, :], in1=wg2_b[:, :],
                                                   scale=-1.0, scalar=0.0, op0=ALU.mult, op1=ALU.add,
                                                   accum_out=c_c[:, g:g + 1]).then_inc(s["dve_a"], 1)

            gates(0, 1)
            dve.wait_ge(s_xT[0], 16)
            x_lo_part(0, 0)

            def body(it):
                t, u = it.t, it.u

                def row_terms(g):
                    dve.wait_ge(s["act_x1n"], nth("act_x1n", u, g))
                    if g > 0:
                        dve.wait_ge(s["dve_r"], nth("dve_r", u, g - 1))
                    else:
                        dve.wait_ge(s["dve_a"], nth("dve_a", t if it.l0 else u, 3))
                    nc.vector.tensor_tensor_reduce(out=scratch[:, :], in0=x1n[:, g, :], in1=v1_b[:, :],
                                                   scale=1.0, scalar=r0_c, op0=ALU.mult, op1=ALU.add,
                                                   accum_out=r_c[:, g:g + 1]).then_inc(s["dve_r"], 1)

                def masked_scores():
                    par_u = 1 - it.par
                    dve.wait_ge(s["dve_r"], nth("dve_r", u, 3))
                    nc.vector.tensor_scalar(flat(mask), flat(adj_sb[par_u]), 0.0, None, ALU.not_equal)
                    nc.vector.tensor_scalar(scratch[:, :], flat(adj_sb[par_u]), 0.0, MASKED, ALU.is_equal,
                                            ALU.mult).then_inc(s["dve_mask"], 1)
                    dve.wait_ge(s["dve_mask"], nth("dve_mask", u))
                    dve.wait_ge(s["pe_sa"], nth("pe_sa", u))
                    for g in range(GG):
                        op = nc.vector.scalar_tensor_tensor(out=att1[:, g, :],
                                                            in0=bank[0][:, g * P:(g + 1) * P],
                                                            scalar=r_c[:, g:g + 1], in1=mask[:, g, :],
                                                            op0=ALU.add, op1=ALU.mult)
                    op.then_inc(s["dve_sa"], 1)
                    dve.wait_ge(s["dve_sa"], nth("dve_sa", u))
                    nc.vector.tensor_tensor(flat(att1), flat(att1), scratch[:, :], ALU.add)\
                      .then_inc(s["dve_sub"], 1)
                    dve.wait_ge(s["dve_sub"], nth("dve_sub", u))
                    nc.vector.tensor_reduce(nmax1, att1[:, :, :], AX.X, ALU.min).then_inc(s["dve_max1"], 1)

                def attention1():
                    dve.wait_ge(s["act_exp1"], nth("act_exp1", u))
                    nc.vector.reciprocal(rcp1, sums1).then_inc(s["dve_rcp1"], 1)
                    dve.wait_ge(s["dve_rcp1"], nth("dve_rcp1", u))
                    for g in range(GG):
                        op = nc.vector.scalar_tensor_tensor(out=att1[:, g, :], in0=att1[:, g, :],
                                                            scalar=rcp1[:, g:g + 1], in1=mask[:, g, :],
                                                            op0=ALU.mult, op1=ALU.mult)
                    op.then_inc(s["dve_att1"], 1)

                def att1T_low():
                    dve.wait_ge(s["act_tp"], nth("act_tp", u))
                    nc.vector.tensor_tensor(flat(att1T_lo), bank[5][:, :], flat(att1T_hi).bitcast(f32),
                                            ALU.subtract).then_inc(s["dve_tp"], 1)

                def y_low(g):
                    dve.wait_ge(s["act_y"], nth("act_y", u, g))
                    nc.vector.tensor_tensor(y_lo[g % 2][:, :], bank[2 + g % 2][:, :],
                                            y_hi[g % 2][:, :].bitcast(f32), ALU.subtract)\
                      .then_inc(s["dve_y"], 1)

                def residual1(g, b):
                    dve.wait_ge(s["pe_ctx"], nth("pe_ctx", u, g))
                    nc.vector.tensor_tensor(x1n[:, g, :], bank[b][:, :], x1n[:, g, :], ALU.add)\
                      .then_inc(s["dve_res"], 1)
                    dve.wait_ge(s["dve_res"], nth("dve_res", u, g))
                    nc.vector.bn_stats(bnst[:, :], x1n[:, g, :]).then_inc(s["dve_bn"], 1)
                    carry_wait(s["dve_bn"], nth("dve_bn", u, g), 2 * C + g)
                    nc.vector.bn_aggr(lnst[:, g, 0:2], bnst[:, :]).then_inc(s["dve_mean"], 1)

                if it.l0:
                    qk_lo(t, 0)
                    bias(t)
                if it.l1:
                    residual0(u, 3, 6, 1 - it.par)
                if it.l0:
                    v_out(t, 0)
                    v_out(t, 1)
                if it.l1:
                    x1lo(u, 3)
                if it.l0:
                    maxima(t, 0)
                    v_out(t, 2)
                    v_out(t, 3)
                    recips(t, 0)
                    qk_lo(t, 1)
                if it.l1:
                    for g in range(GG):
                        row_terms(g)
                if it.l0:
                    maxima(t, 1)
                if it.l1:
                    masked_scores()
                if it.l0:
                    recips(t, 1)
                if it.l1:
                    y_low(0)
                    attention1()
                    y_low(1)
                if it.l0:
                    qk_lo(t, 2)
                if it.l1:
                    att1T_low()
                    residual1(0, 0)
                    residual1(1, 1)
                    y_low(2)
                    y_low(3)
                if not it.l1:
                    dve.wait_ge(s_whi, 8)
                    nc.vector.tensor_tensor(flat(w_lo["c"]), flat(x1T), flat(w_hi["c"]).bitcast(f32),
                                            ALU.subtract).then_inc(s_wlo, 1)
                    dve.wait_ge(s_wlo, 8)
                if it.l0:
                    residual0(t, 0, 6, it.par)
                    maxima(t, 2)
                    residual0(t, 1, 7, it.par)
                    x1lo(t, 0)
                    x1lo(t, 1)
                    recips(t, 2)
                    qk_lo(t, 3)
                if it.nxt:
                    dve.wait_ge(s_xT[1 - it.par], 16 * (it.p + 1 + it.par))
                    x_lo_part(t + 1, 1 - it.par)
                if it.l1:
                    residual1(2, 2)
                    residual1(3, 3)
                if it.nxt:
                    gates(t + 1, 2 * t + 3)
                if it.l0:
                    maxima(t, 3)
                    residual0(t, 2, 6, it.par)
                    recips(t, 3)
                    x1lo(t, 2)

            iterations(dve, body)

        @block.gpsimd
        def _(pool):
            nc.gpsimd.memset(k_hi[:, :, :].bitcast(f32), 0.0)
            nc.gpsimd.memset(k_lo[:, :, :].bitcast(f32), 0.0).then_inc(s_zero, 1)

            pool.wait_ge(s_half, 1)

            def probabilities(t, c):
                for h in range(2):
                    half = slice(h * HALF, (h + 1) * HALF)
                    pool.wait_ge(s["dve_rcp"], nth("dve_rcp", t, 2 * c + h))
                    nc.gpsimd.tensor_tensor(probs[:, half, :], probs[:, half, :],
                                            rcp[:, half].unsqueeze(2).to_broadcast([P, HALF, P]), ALU.mult)\
                        .then_inc(s["pool_p"], 1)

            def body(it):
                t, u = it.t, it.u

                def sigma(g):
                    pool.wait_ge(s["dve_mean"], nth("dve_mean", u, g))
                    nc.gpsimd.tensor_tensor(lnst[:, g, 0:1], lnst[:, g, 0:1], minus_c, ALU.mult)
                    nc.gpsimd.tensor_tensor(lnst[:, g, 3:4], lnst[:, g, 1:2], eps1_c, ALU.add)\
                        .then_inc(s["pool_eps"], 1)
                    pool.wait_ge(s["pool_eps"], nth("pool_eps", u, g))
                    nc.gpsimd.tensor_tensor(lnst[:, g, 2:3], lnst[:, g, 3:4], half_c, ALU.pow)\
                        .then_inc(s["pool_rstd"], 1)
                    pool.wait_ge(s["pool_rstd"], nth("pool_rstd", u, g))
                    nc.gpsimd.tensor_tensor(lnst[:, g, 3:4], lnst[:, g, 0:1], lnst[:, g, 2:3], ALU.mult)\
                        .then_inc(s["pool_nmr"], 1)

                def affine(g):
                    pool.wait_ge(s["act_nrm"], nth("act_nrm", u, g))
                    nc.gpsimd.tensor_tensor(x1n[:, g, :], x1n[:, g, :], gamma_b[:, :], ALU.mult)\
                        .then_inc(s["pool_gam"], 1)
                    pool.wait_ge(s["pool_gam"], nth("pool_gam", u, g))
                    nc.gpsimd.tensor_tensor(x1n[:, g, :], x1n[:, g, :], beta_b[:, :], ALU.add)\
                        .then_inc(s["pool_out"], 1)

                if it.l1:
                    probabilities(u, 3)
                if it.l0:
                    probabilities(t, 0)
                    probabilities(t, 1)
                if it.l1:
                    for g in range(2):
                        sigma(g)
                    for g in range(2):
                        affine(g)
                if it.l0:
                    probabilities(t, 2)
                if it.l1:
                    for g in range(2, 4):
                        sigma(g)
                    for g in range(2, 4):
                        affine(g)

            iterations(pool, body)



def kernel(x, adj, L0_gnn_W_q, L0_gnn_b_q, L0_gnn_W_k, L0_gnn_b_k, L0_gnn_W_v, L0_gnn_b_v, L0_gnn_w_g,
           L0_gnn_b_g, L1_gnn_Wq, L1_gnn_bq, L1_gnn_Wk, L1_gnn_bk, L1_gnn_Wc, L1_gnn_gamma,
           L1_gnn_beta):
    import numpy as np
    import concourse.bacc as bacc
    from concourse import mybir as mb
    from concourse.bass_utils import run_bass_kernel_spmd

    def host(a):
        return np.asarray(a)

    def chunks(w):
        return host(w).reshape(C, P, -1).transpose(1, 0, 2)

    xs = host(x)
    arrays = {
        "xT": xs.reshape(NG, COLS, C, P).transpose(0, 3, 2, 1).reshape(NG * P, C * COLS),
        "x": xs.reshape(GRAPHS * P, D),
        "adj": host(adj),
        "wq": chunks(L0_gnn_W_q), "wk": chunks(L0_gnn_W_k), "wv": chunks(L0_gnn_W_v),
        "wqT1": chunks(host(L1_gnn_Wq).T), "wkT1": chunks(host(L1_gnn_Wk).T), "wc": chunks(L1_gnn_Wc),
        "bq0": host(L0_gnn_b_q).reshape(C, P).T, "bk0": host(L0_gnn_b_k).reshape(C, P).T,
        "bv0": host(L0_gnn_b_v).reshape(1, D), "wg": host(L0_gnn_w_g).reshape(1, 2 * D),
        "bg": host(L0_gnn_b_g).reshape(1, 1),
        "bq1": host(L1_gnn_bq).reshape(C, P).T, "bk1": host(L1_gnn_bk).reshape(C, P).T,
        "gamma": host(L1_gnn_gamma).reshape(1, D), "beta": host(L1_gnn_beta).reshape(1, D),
        "ident_in": np.eye(P, dtype=np.float32),
    }
    arrays = {n: np.ascontiguousarray(a) for n, a in arrays.items()}
    nc = bacc.Bacc("TRN2", target_bir_lowering=False, num_devices=1, dynamic_dma_scratch_size=1024)
    ins = {n: nc.dram_tensor(f"in_{n}", a.shape, mb.dt.from_np(a.dtype), kind="ExternalInput").ap()
           for n, a in arrays.items()}
    out = nc.dram_tensor("out", (GRAPHS * P, D), mb.dt.float32, kind="ExternalOutput").ap()
    gnn_program(nc, out=out, **ins)
    r = run_bass_kernel_spmd(nc, [{f"in_{n}": a for n, a in arrays.items()}], core_ids=[0])
    return r.results[0]["out"].reshape(GRAPHS, P, D)
```

```python
from collections import namedtuple
from contextlib import ExitStack

import concourse.bass as bass
from concourse import mybir

P = 128
GRAPHS = 128
D = 512
HEADS = 8
HD = D // HEADS
C = D // P
GG = 4
NG = GRAPHS // GG
COLS = GG * P
PAIR = 2 * GG
HALF = PAIR // 2
EPS_ADJ = 1e-9
EPS_LN = 1e-5
MASKED = 1e18
SCALE0 = float(HD) ** -0.5
SCALE1 = float(D) ** -0.5
BIG = 3.0e38


Iteration = namedtuple("Iteration", "t u p par l0 l1 second nxt")


def gnn_program(nc, xT, x, adj, wq, wk, wv, wqT1, wkT1, wc, bq0, bk0, bv0, wg, bg, bq1, bk1,
                gamma, beta, ident_in, out):
    f32 = mybir.dt.float32
    f32r = mybir.dt.float32r
    bf16 = mybir.dt.bfloat16
    ALU = mybir.AluOpType
    ACT = mybir.ActivationFunctionType
    AX = mybir.AxisListType

    adj_v = adj.rearrange("g i j -> i g j")

    with ExitStack() as ctx:
        def sb(name, shape, dt=f32):
            return ctx.enter_context(nc.sbuf_tensor(name, shape, dt))

        def sem(name):
            return ctx.enter_context(nc.semaphore(name))

        w_hi = {n: sb(f"w{n}_hi", [P, C, D], f32r) for n in "qkvmc"}
        w_lo = {n: sb(f"w{n}_lo", [P, C, D], f32r) for n in "qkvmc"}
        xT_land = [sb(f"xT_land{i}", [P, C, COLS]) for i in range(2)]
        x_hi = sb("x_hi", [P, C, COLS], f32r)
        x_lo = sb("x_lo", [P, C, COLS], f32r)
        q_hi = sb("q_hi", [P, COLS], f32r)
        q_lo = sb("q_lo", [P, COLS], f32r)
        k_hi = sb("k_hi", [P, GG, 2 * P], f32r)
        k_lo = sb("k_lo", [P, GG, 2 * P], f32r)
        v_sb = sb("v_sb", [P, GG, D])
        probs = sb("probs", [P, PAIR, P])
        probsT = [sb(f"probsT{i}", [P, PAIR, P]) for i in range(2)]
        x1T = sb("x1T", [P, C, COLS])
        x1_hi = sb("x1_hi", [P, C, COLS], f32r)
        x1_lo = sb("x1_lo", [P, C, COLS], f32r)
        g_sb = [sb(f"g_sb{i}", [P, COLS]) for i in range(2)]
        y_hi = [sb(f"y_hi{i}", [P, D], f32r) for i in range(2)]
        y_lo = [sb(f"y_lo{i}", [P, D], f32r) for i in range(2)]
        x1n = sb("x1n", [P, GG, D])
        xn = [sb(f"xn{i}", [P, D]) for i in range(2)]
        adj_sb = [sb(f"adj_sb{i}", [P, GG, P]) for i in range(2)]
        ln_adj = sb("ln_adj", [P, GG, P])
        bias0 = sb("bias0", [P, GG, P])
        mask = sb("mask", [P, GG, P], bf16)
        att1 = sb("att1", [P, GG, P])
        att1T_hi = sb("att1T_hi", [P, GG, P], f32r)
        att1T_lo = sb("att1T_lo", [P, GG, P], f32r)
        scratch = sb("scratch", [P, D])
        bv_b = sb("bv_b", [P, D])
        gamma_b = sb("gamma_b", [P, D])
        beta_b = sb("beta_b", [P, D])
        wg1_b = sb("wg1_b", [P, D])
        wg2_b = sb("wg2_b", [P, D])
        v1_b = sb("v1_b", [P, D])
        ident = sb("ident", [P, P])
        cols = sb("cols", [P, 4 * C])
        bq0_c, bk0_c, bq1_c, bk1_c = (cols[:, C * i:C * (i + 1)] for i in range(4))
        consts = sb("consts", [P, 16])
        bg_c, nbg_c, r0_c, half_c, eps_c, eps1_c, minus_c = (consts[:, i:i + 1] for i in range(7))
        u1_c = consts[:, 8:8 + C]
        nbq0_c = consts[:, 12:12 + C]
        carrier = sb("carrier", [P, 2 * C + GG])
        a_c = sb("a_c", [P, GG])
        c_c = sb("c_c", [P, GG])
        r_c = sb("r_c", [P, GG])
        nmax = sb("nmax", [P, PAIR])
        sums = sb("sums", [P, PAIR])
        rcp = sb("rcp", [P, PAIR])
        stats1 = sb("stats1", [P, 3 * GG])
        nmax1, sums1, rcp1 = (stats1[:, GG * i:GG * (i + 1)] for i in range(3))
        bnst = sb("bnst", [P, 6])
        lnst = sb("lnst", [P, GG, 4])

        bank = [ctx.enter_context(nc.psum_tensor(f"bank{i}", [P, 512], f32)) for i in range(8)]

        PER = dict(pe_q=4, pe_k=4, pe_cb=1, pe_s=8, pe_t=8, pe_v=4, pe_pv=4, pe_g=4, pe_x=4, pe_sa=1,
                   pe_y=4, pe_tp=1, pe_ctx=4,
                   act_q=4, act_k=4, act_exp=2 * C, act_pt=2 * C, act_x1=4, act_g=4, act_x1n=4,
                   act_y=4, act_ln=1, act_exp1=1, act_tp=1, act_nrm=4,
                   dve_q=4, dve_k=4, dve_b=1, dve_max=2 * C, dve_rcp=2 * C, dve_v=4, dve_pv=4,
                   dve_x1=4, dve_a=4, dve_r=4, dve_mask=1, dve_sa=1, dve_sub=1, dve_max1=1,
                   dve_rcp1=1, dve_att1=1, dve_tp=1, dve_y=4, dve_res=4, dve_bn=4, dve_mean=4,
                   dve_x=4, act_x=4, pool_p=2 * C, pool_eps=4, pool_rstd=4, pool_nmr=4,
                   pool_gam=4, pool_out=4)
        s = {n: sem(n) for n in PER}
        s_xT = [sem(f"xT_loaded{i}") for i in range(2)]
        s_adj = [sem(f"adj_loaded{i}") for i in range(2)]
        s_xn = [sem(f"xn_loaded{i}") for i in range(2)]
        s_out = [sem(f"out_stored{i}") for i in range(GG)]
        s_wld = {n: sem(f"w{n}_loaded") for n in ("q", "k", "v", "q1", "k1", "c")}
        s_const = sem("const_loaded")
        s_zero = sem("pool_zeroed")
        s_whi = sem("act_w_hi")
        s_wlo = sem("dve_w_lo")
        s_m = sem("pe_m")
        m_banks = (2, 3, 6, 7)
        s_const1 = sem("const1_loaded")
        s_cst = sem("dve_const")
        s_half = sem("dve_half")

        def nth(name, t, k=0):
            return t * PER[name] + k + 1

        def y_bank(g):
            return (2, 3, 0, 1)[g]

        def hi_lo(out_ap, st, mv):
            for i in range(len(st)):
                last = hi_lo_part(out_ap, st[i], mv[i], i == 0, i == len(st) - 1)
            return last

        def hi_lo_part(out_ap, st, mv, start, stop):
            nc.tensor.matmul(out_ap, st[0], mv[0], start=start, stop=False)
            nc.tensor.matmul(out_ap, st[0], mv[1], start=False, stop=False)
            return nc.tensor.matmul(out_ap, st[1], mv[0], start=False, stop=stop)

        def w_cols(n, c):
            return [(w_hi[n][:, d, c * P:(c + 1) * P], w_lo[n][:, d, c * P:(c + 1) * P]) for d in range(C)]

        def w_rows(n):
            return [(w_hi[n][:, d, :], w_lo[n][:, d, :]) for d in range(C)]

        def act_cols(hi, lo):
            return [(hi[:, d, :], lo[:, d, :]) for d in range(C)]

        def act_rows(hi, lo, g):
            return [(hi[:, d, g * P:(g + 1) * P], lo[:, d, g * P:(g + 1) * P]) for d in range(C)]

        def flat(t):
            return t[:, :, :].rearrange("p a b -> p (a b)")


        def iterations(eng, body):
            def step(p, par, **kinds):
                t = 2 * p + par
                body(Iteration(**{**dict(t=t, u=t - 1, p=p, par=par, l0=True, l1=True, second=False,
                                         nxt=True), **kinds}))
            step(0, 0, l1=False)
            step(0, 1, second=True)
            with eng.Fori(1, NG // 2 - 1) as p:
                step(p, 0)
                step(p, 1)
            step(NG // 2 - 1, 0)
            step(NG // 2 - 1, 1, nxt=False)
            step(NG // 2, 0, l0=False, nxt=False)

        block = ctx.enter_context(nc.Block())

        @block.sync
        def _(sp):
            def load_xT(t, par):
                sp.dma_start(flat(xT_land[par]), xT[bass.ds(t * P, P), :]).then_inc(s_xT[par], 16)

            def load_adj(t, par):
                sp.dma_start(adj_sb[par][:, :, :], adj_v[:, bass.ds(t * GG, GG), :]).then_inc(s_adj[par], 16)

            def load_xn(t, g):
                sp.dma_start(xn[g % 2][:, :], x[bass.ds(t * COLS + g * P, P), :]).then_inc(s_xn[g % 2], 16)

            sp.dma_start(ident[:, :], ident_in).then_inc(s_const1, 16)
            sp.dma_start(bq1_c, bq1).then_inc(s_const1, 16)
            sp.dma_start(bk1_c, bk1).then_inc(s_const1, 16)
            sp.dma_start(x1T[:, :, :], wqT1).then_inc(s_wld["q1"], 16)
            sp.dma_start(x1n[:, :, :], wkT1).then_inc(s_wld["k1"], 16)
            sp.dma_start(xT_land[1][:, :, :], wq).then_inc(s_wld["q"], 16)
            sp.dma_start(v_sb[:, :, :], wk).then_inc(s_wld["k"], 16)
            load_xT(0, 0)
            for i in range(2):
                sp.dma_start(flat(probsT[i]), wv[:, 2 * i:2 * i + 2, :].rearrange("p a b -> p (a b)"))\
                  .then_inc(s_wld["v"], 16)
            sp.dma_start(bq0_c, bq0).then_inc(s_const, 16)
            sp.dma_start(bk0_c, bk0).then_inc(s_const, 16)
            sp.dma_start(bg_c, bg.to_broadcast([P, 1])).then_inc(s_const, 16)
            sp.dma_start(wg1_b[:, :], wg[:, 0:D].to_broadcast([P, D])).then_inc(s_const, 16)
            sp.dma_start(wg2_b[:, :], wg[:, D:2 * D].to_broadcast([P, D])).then_inc(s_const, 16)
            sp.dma_start(bv_b[:, :], bv0.to_broadcast([P, D])).then_inc(s_const, 16)
            sp.dma_start(gamma_b[:, :], gamma.to_broadcast([P, D])).then_inc(s_const, 16)
            sp.dma_start(beta_b[:, :], beta.to_broadcast([P, D])).then_inc(s_const, 16)
            load_adj(0, 0)
            load_xn(0, 0)
            load_xn(0, 1)
            sp.wait_ge(s["dve_a"], nth("dve_a", 0, 0))
            load_xn(0, 2)
            sp.wait_ge(s["dve_a"], nth("dve_a", 0, 1))
            load_xn(0, 3)
            sp.wait_ge(s_m, C + 1)
            sp.dma_start(x1T[:, :, :], wc).then_inc(s_wld["c"], 16)

            def body(it):
                t, u = it.t, it.u
                if it.nxt:
                    if it.l1:
                        sp.wait_ge(s["dve_pv"], nth("dve_pv", u, 3))
                    else:
                        sp.wait_ge(s_wlo, 1)
                    load_xT(t + 1, 1 - it.par)
                    for g in range(2):
                        sp.wait_ge(s["dve_a"], nth("dve_a", t, g + 2))
                        load_xn(t + 1, g)
                    if it.l1:
                        sp.wait_ge(s["dve_mask"], nth("dve_mask", u))
                    load_adj(t + 1, 1 - it.par)

                def store(g):
                    sp.wait_ge(s["pool_out"], nth("pool_out", u, g))
                    sp.dma_start(out[bass.ds(u * COLS + g * P, P), :], x1n[:, g, :]).then_inc(s_out[g], 16)

                if it.nxt:
                    for g in range(2, 4):
                        sp.wait_ge(s["dve_a"], nth("dve_a", t + 1, g - 2))
                        load_xn(t + 1, g)
                if it.l1:
                    for g in range(GG):
                        store(g)

            iterations(sp, body)
            for g in range(GG):
                sp.wait_ge(s_out[g], 16 * NG)

        @block.tensor
        def _(pe):
            pe.wait_ge(s_wld["q1"], 16)
            pe.wait_ge(s_wld["k1"], 16)
            pe.wait_ge(s_const1, 16 * 3)
            for d in range(C):
                for f in range(C):
                    mm = nc.tensor.matmul(bank[m_banks[d]][:, :], x1T[:, f, d * P:(d + 1) * P], x1n[:, f, :],
                                          start=(f == 0), stop=(f == C - 1))
                mm.then_inc(s_m, 1)
            for f in range(C):
                mm = nc.tensor.matmul(bank[4][:, :], bk1_c[:, f:f + 1].to_broadcast([P, P]), x1T[:, f, :],
                                      start=(f == 0), stop=(f == C - 1))
            for f in range(C):
                mm = nc.tensor.matmul(bank[5][:, 0:1], bk1_c[:, f:f + 1].to_broadcast([P, P]),
                                      bq1_c[:, f:f + 1], start=(f == 0), stop=(f == C - 1))
            for d in range(C):
                for f in range(C):
                    mm = nc.tensor.matmul(bank[5][:, 1 + d:2 + d], x1n[:, f, d * P:(d + 1) * P],
                                          bq1_c[:, f:f + 1], start=(f == 0), stop=(f == C - 1))
            mm.then_inc(s_m, 1)

            def project_k(t, c):
                for d in range(C):
                    if c == 0:
                        pe.wait_ge(s["dve_x"], nth("dve_x", t, d))
                    mm = hi_lo_part(bank[1][:, :], w_cols("k", c)[d], act_cols(x_hi, x_lo)[d], d == 0, d == C - 1)
                mm.then_inc(s["pe_k"], 1)

            def project_q(t, c):
                hi_lo(bank[0][:, :], w_cols("q", c), act_cols(x_hi, x_lo)).then_inc(s["pe_q"], 1)

            def v(t, g, first, second):
                if g < 2 and not first and not second:
                    pe.wait_ge(s["dve_res"], nth("dve_res", t - 2, g + 2))
                if g < 2 and second:
                    pe.wait_ge(s["dve_v"], nth("dve_v", t - 1, g + 2))
                if g >= 2:
                    pe.wait_ge(s["dve_v"], nth("dve_v", t, g - 2))
                hi_lo(bank[2 + g % 2][:, :], act_rows(x_hi, x_lo, g), w_rows("v")).then_inc(s["pe_v"], 1)

            def scores(t, c):
                pe.wait_ge(s["dve_q"], nth("dve_q", t, c))
                pe.wait_ge(s["dve_k"], nth("dve_k", t, c))
                for g in range(GG):
                    if g == 0 and c > 0:
                        pe.wait_ge(s["dve_max"], nth("dve_max", t, 2 * c - 2))
                    if g == 2 and c > 0:
                        pe.wait_ge(s["dve_max"], nth("dve_max", t, 2 * c - 1))
                    if g == 2 and c == 0:
                        pe.wait_ge(s["dve_b"], nth("dve_b", t))
                    cols_g = slice(g * P, (g + 1) * P)
                    mm = hi_lo(bank[4 + g // 2][:, (g % 2) * 2 * P:(g % 2 + 1) * 2 * P],
                               [(q_hi[:, cols_g], q_lo[:, cols_g])], [(k_hi[:, g, :], k_lo[:, g, :])])
                    if g % 2:
                        mm.then_inc(s["pe_s"], 1)

            def turn(t, c):
                for h in range(2):
                    pe.wait_ge(s["pool_p"], nth("pool_p", t, 2 * c + h))
                    for k in range(HALF):
                        mm = nc.tensor.transpose(bank[6 + h][:, k * P:(k + 1) * P],
                                                 probs[:, h * HALF + k, :], ident[:, :])
                    mm.then_inc(s["pe_t"], 1)

            def pv(t, c, b):
                for h in range(2):
                    pe.wait_ge(s["act_pt"], nth("act_pt", t, 2 * c + h))
                    if c == 0 and h == 0:
                        pe.wait_ge(s["dve_v"], nth("dve_v", t, GG - 1))
                    for g in range(2 * h, 2 * h + 2):
                        for e in range(2):
                            mm = nc.tensor.matmul(bank[b][e * HD:(e + 1) * HD, g * P:(g + 1) * P],
                                                  v_sb[:, g, c * P + e * HD:c * P + (e + 1) * HD],
                                                  probsT[c % 2][:, 2 * g + e, :], start=True, stop=True)
                mm.then_inc(s["pe_pv"], 1)

            def body(it):
                t, u = it.t, it.u
                first, second, last = not it.l1, it.second, not it.l0
                if not last:
                    if first:
                        pe.wait_ge(s_wlo, 2)
                    else:
                        pe.wait_ge(s["dve_k"], nth("dve_k", t - 1, 3))
                    project_k(t, 0)
                    if not first:
                        pe.wait_ge(s["dve_q"], nth("dve_q", t - 1, 3))
                    project_q(t, 0)
                    if not first:
                        pe.wait_ge(s["dve_max"], nth("dve_max", t - 1, 2 * C - 1))
                    else:
                        pe.wait_ge(s_cst, 1)
                    pe.wait_ge(s["dve_a"], nth("dve_a", t, 3))
                    for g in range(GG):
                        mm = nc.tensor.transpose(bank[5][:, g * P:(g + 1) * P],
                                                 c_c[:, g:g + 1].to_broadcast([P, P]), ident[:, :])
                    mm.then_inc(s["pe_cb"], 1)
                    if first:
                        pe.wait_ge(s_wlo, 7)
                    v(t, 0, first, second)
                if not first:
                    pe.wait_ge(s["dve_pv"], nth("dve_pv", u, 2))
                    pe.wait_ge(s["act_pt"], nth("act_pt", u, 5))
                    turn(u, 3)
                if not last:
                    v(t, 1, first, second)
                if not first:
                    pv(u, 3, 6)
                if not last:
                    scores(t, 0)
                    v(t, 2, first, second)
                    v(t, 3, first, second)
                    project_k(t, 1)
                    project_q(t, 1)

                def gw(c):
                    if c < 2:
                        if not last:
                            pe.wait_ge(s["dve_v"], nth("dve_v", t, c + 2))
                        else:
                            pe.wait_ge(s["dve_res"], nth("dve_res", u - 1, c + 2))
                        if c == 0:
                            pe.wait_ge(s["dve_x1"], nth("dve_x1", u, 3))
                            if second:
                                pe.wait_ge(s_wlo, 8)
                    else:
                        pe.wait_ge(s["act_g"], nth("act_g", u, c - 2))
                    hi_lo(bank[2 + c % 2][:, :], w_cols("m", c), act_cols(x1_hi, x1_lo)).then_inc(s["pe_g"], 1)

                def xw(g):
                    if g == 0:
                        if not last:
                            pe.wait_ge(s["dve_k"], nth("dve_k", t, 1))
                        else:
                            pe.wait_ge(s["dve_k"], nth("dve_k", u, 3))
                    else:
                        pe.wait_ge(s["act_x1n"], nth("act_x1n", u, g - 1))
                    for d in range(C):
                        mm = nc.tensor.transpose(bank[1][:, d * P:(d + 1) * P],
                                                 x1T[:, d, g * P:(g + 1) * P], ident[:, :])
                    mm.then_inc(s["pe_x"], 1)

                def sa(c):
                    if c == 0:
                        if not last:
                            pe.wait_ge(s["dve_q"], nth("dve_q", t, 1))
                        else:
                            pe.wait_ge(s["dve_q"], nth("dve_q", u, 3))
                    pe.wait_ge(s["act_g"], nth("act_g", u, c))
                    for g in range(GG):
                        cols_g = slice(g * P, (g + 1) * P)
                        mm = nc.tensor.matmul(bank[0][:, cols_g], g_sb[c % 2][:, cols_g], x1T[:, c, cols_g],
                                              start=(c == 0 and g == 0), stop=(c == C - 1),
                                              skip_group_check=True)
                    if c == C - 1:
                        mm.then_inc(s["pe_sa"], 1)

                def yw(g):
                    if g < 2:
                        pe.wait_ge(s["act_g"], nth("act_g", u, g + 2))
                    hi_lo(bank[y_bank(g)][:, :], act_rows(x1_hi, x1_lo, g), w_rows("c")).then_inc(s["pe_y"], 1)

                def cx(g, b):
                    pe.wait_ge(s["dve_y"], nth("dve_y", u, g))
                    hi_lo(bank[b][:, :], [(att1T_hi[:, g, :], att1T_lo[:, g, :])],
                          [(y_hi[g % 2][:, :], y_lo[g % 2][:, :])]).then_inc(s["pe_ctx"], 1)

                if not first:
                    gw(0)
                    xw(0)
                    gw(1)
                    xw(1)
                if not last:
                    if not first:
                        pe.wait_ge(s["dve_pv"], nth("dve_pv", u, 3))
                        pe.wait_ge(s["act_pt"], nth("act_pt", u, 7))
                    turn(t, 0)
                if not first:
                    sa(0)
                    gw(2)
                    xw(2)
                    sa(1)
                    gw(3)
                    xw(3)
                    sa(2)
                if not last:
                    scores(t, 1)
                if not first:
                    sa(3)
                    yw(0)
                    yw(1)
                if not last:
                    if not first:
                        pe.wait_ge(s["act_x1n"], nth("act_x1n", u, 3))
                    project_k(t, 2)
                    if not first:
                        pe.wait_ge(s["dve_sa"], nth("dve_sa", u))
                if not first:
                    if not last:
                        pe.wait_ge(s["dve_max"], nth("dve_max", t, 3))
                    else:
                        pe.wait_ge(s["dve_max"], nth("dve_max", u, 7))
                    pe.wait_ge(s["dve_att1"], nth("dve_att1", u))
                    for g in range(GG):
                        mm = nc.tensor.transpose(bank[5][:, g * P:(g + 1) * P], att1[:, g, :], ident[:, :])
                    mm.then_inc(s["pe_tp"], 1)
                if not last:
                    project_q(t, 2)
                    pe.wait_ge(s["act_pt"], nth("act_pt", t, 1))
                    turn(t, 1)
                if not first:
                    pe.wait_ge(s["dve_tp"], nth("dve_tp", u))
                    cx(0, 2)
                    cx(1, 3)
                    if not last:
                        pe.wait_ge(s["dve_q"], nth("dve_q", t, 2))
                    else:
                        pe.wait_ge(s["dve_sa"], nth("dve_sa", u))
                    yw(2)
                    if not last:
                        pe.wait_ge(s["dve_k"], nth("dve_k", t, 2))
                    else:
                        pe.wait_ge(s["act_x1n"], nth("act_x1n", u, 3))
                    yw(3)
                if not last:
                    pe.wait_ge(s["act_pt"], nth("act_pt", t, 2))
                    pv(t, 0, 6)
                    if not first:
                        pe.wait_ge(s["dve_tp"], nth("dve_tp", u))
                    scores(t, 2)
                    pe.wait_ge(s["act_pt"], nth("act_pt", t, 3))
                    pv(t, 1, 7)
                    if not first:
                        pe.wait_ge(s["dve_y"], nth("dve_y", u, 3))
                    project_k(t, 3)
                    project_q(t, 3)
                if not first:
                    pe.wait_ge(s["dve_res"], nth("dve_res", u, 1))
                    cx(2, 2)
                if not last:
                    pe.wait_ge(s["dve_pv"], nth("dve_pv", t, 0))
                    pe.wait_ge(s["dve_pv"], nth("dve_pv", t, 1))
                    turn(t, 2)
                if not first:
                    cx(3, 3)
                if not last:
                    scores(t, 3)
                    pv(t, 2, 6)

            iterations(pe, body)

        @block.scalar
        def _(act):
            act.wait_ge(s_wld["q"], 16)
            nc.scalar.activation(w_hi["q"][:, :, :], xT_land[1][:, :, :], ACT.Copy, scale=-SCALE0)\
              .then_inc(s_whi, 1)
            act.wait_ge(s_wld["k"], 16)
            nc.scalar.activation(w_hi["k"][:, :, :], v_sb[:, :, :], ACT.Copy).then_inc(s_whi, 1)
            def x_hi_chunk(par, c):
                nc.scalar.activation(x_hi[:, c, :], xT_land[par][:, c, :], ACT.Copy).then_inc(s["act_x"], 1)

            act.wait_ge(s_xT[0], 16)
            for c in range(C):
                x_hi_chunk(0, c)
            act.wait_ge(s_wld["v"], 32)
            for i in range(2):
                op = nc.scalar.activation(w_hi["v"][:, 2 * i:2 * i + 2, :].rearrange("p a b -> p (a b)"),
                                          flat(probsT[i]), ACT.Copy)
            op.then_inc(s_whi, 1)
            for d in range(C):
                act.wait_ge(s_m, d + 1)
                nc.scalar.activation(w_hi["m"][:, d, :], bank[m_banks[d]][:, :], ACT.Copy, scale=-SCALE1)\
                  .then_inc(s_whi, 1)
            act.wait_ge(s_cst, 1)
            act.wait_ge(s_zero, 1)

            def log_adj(t, loads, par):
                act.wait_ge(s_adj[par], 16 * loads)
                nc.scalar.activation(ln_adj[:, :, :], adj_sb[par][:, :, :], ACT.Ln,
                                     bias=eps_c).then_inc(s["act_ln"], 1)

            log_adj(0, 1, 0)

            def k_high(t, c):
                act.wait_ge(s["pe_k"], nth("pe_k", t, c))
                for e in range(2):
                    r = slice(e * HD, (e + 1) * HD)
                    op = nc.scalar.activation(k_hi[r, :, e * P:(e + 1) * P],
                                              bank[1][r, :].rearrange("p (g j) -> p g j", g=GG),
                                              ACT.Identity, bias=bk0_c[r, c:c + 1])
                op.then_inc(s["act_k"], 1)

            def q_high(t, c):
                act.wait_ge(s["pe_q"], nth("pe_q", t, c))
                nc.scalar.activation(q_hi[:, :], bank[0][:, :], ACT.Identity,
                                     bias=nbq0_c[:, c:c + 1]).then_inc(s["act_q"], 1)

            def exps(t, c):
                for h in range(2):
                    act.wait_ge(s["dve_max"], nth("dve_max", t, 2 * c + h))
                    for k in range(h * HALF, (h + 1) * HALF):
                        op = nc.scalar.activation(probs[:, k, :], probs[:, k, :], ACT.Exp,
                                                  bias=nmax[:, k:k + 1], scale=-1.0,
                                                  accum_out=sums[:, k:k + 1])
                    op.then_inc(s["act_exp"], 1)

            def turned(t, c):
                for h in range(2):
                    act.wait_ge(s["pe_t"], nth("pe_t", t, 2 * c + h))
                    nc.scalar.activation(probsT[c % 2][:, h * HALF:(h + 1) * HALF, :]
                                         .rearrange("p a b -> p (a b)"),
                                         bank[6 + h][:, :], ACT.Copy).then_inc(s["act_pt"], 1)

            def x1hi(t, c):
                act.wait_ge(s["dve_pv"], nth("dve_pv", t, c))
                nc.scalar.activation(x1_hi[:, c, :], x1T[:, c, :], ACT.Copy).then_inc(s["act_x1"], 1)

            def body(it):
                t, u = it.t, it.u

                def g_out(c):
                    act.wait_ge(s["pe_g"], nth("pe_g", u, c))
                    nc.scalar.activation(g_sb[c % 2][:, :], bank[2 + c % 2][:, :], ACT.Identity,
                                         bias=u1_c[:, c:c + 1]).then_inc(s["act_g"], 1)

                def x1_out(g):
                    act.wait_ge(s["pe_x"], nth("pe_x", u, g))
                    if not it.second:
                        act.wait_ge(s_out[g], 16 * u)
                    nc.scalar.activation(x1n[:, g, :], bank[1][:, :], ACT.Copy).then_inc(s["act_x1n"], 1)

                def y_out(g):
                    act.wait_ge(s["pe_y"], nth("pe_y", u, g))
                    nc.scalar.activation(y_hi[g % 2][:, :], bank[y_bank(g)][:, :], ACT.Copy)\
                      .then_inc(s["act_y"], 1)

                def norm(u, g):
                    act.wait_ge(s["pool_nmr"], nth("pool_nmr", u, g))
                    nc.scalar.activation(x1n[:, g, :], x1n[:, g, :], ACT.Identity,
                                         bias=lnst[:, g, 3:4], scale=lnst[:, g, 2:3]).then_inc(s["act_nrm"], 1)

                if it.l0:
                    k_high(t, 0)
                    q_high(t, 0)
                if it.l1:
                    turned(u, 3)
                    if not it.second:
                        norm(u - 1, 3)
                    x1hi(u, 3)
                if it.l0:
                    exps(t, 0)
                    k_high(t, 1)
                    q_high(t, 1)
                if it.l1:
                    g_out(0)
                    x1_out(0)
                    g_out(1)
                    x1_out(1)
                if it.l0:
                    turned(t, 0)
                if it.l1:
                    g_out(2)
                    x1_out(2)
                    g_out(3)
                    x1_out(3)
                if it.l0:
                    exps(t, 1)
                if it.l1:
                    act.wait_ge(s["dve_max1"], nth("dve_max1", u))
                    for g in range(GG):
                        op = nc.scalar.activation(att1[:, g, :], att1[:, g, :], ACT.Exp,
                                                  bias=nmax1[:, g:g + 1], scale=-1.0,
                                                  accum_out=sums1[:, g:g + 1])
                    op.then_inc(s["act_exp1"], 1)
                    y_out(0)
                    y_out(1)
                if it.l0:
                    k_high(t, 2)
                if it.l1:
                    act.wait_ge(s["pe_tp"], nth("pe_tp", u))
                    nc.scalar.activation(flat(att1T_hi), bank[5][:, :], ACT.Copy).then_inc(s["act_tp"], 1)
                if it.l0:
                    q_high(t, 2)
                    turned(t, 1)
                if it.l1:
                    y_out(2)
                    norm(u, 0)
                    y_out(3)
                    norm(u, 1)
                if not it.l1:
                    act.wait_ge(s_wld["c"], 16)
                    nc.scalar.activation(w_hi["c"][:, :, :], x1T[:, :, :], ACT.Copy).then_inc(s_whi, 1)
                if it.l0:
                    x1hi(t, 0)
                    exps(t, 2)
                    x1hi(t, 1)
                    k_high(t, 3)
                    q_high(t, 3)
                if it.nxt:
                    act.wait_ge(s["pe_q"], nth("pe_q", t, C - 1))
                    act.wait_ge(s_xT[1 - it.par], 16 * (it.p + 1 + it.par))
                    x_hi_chunk(1 - it.par, 0)
                    x_hi_chunk(1 - it.par, 1)
                if it.l0:
                    turned(t, 2)
                if it.nxt:
                    x_hi_chunk(1 - it.par, 2)
                    x_hi_chunk(1 - it.par, 3)
                if it.l0:
                    exps(t, 3)
                    x1hi(t, 2)
                if it.nxt:
                    act.wait_ge(s["dve_b"], nth("dve_b", t))
                    log_adj(t + 1, it.p + 1 + it.par, 1 - it.par)
                if it.l1:
                    norm(u, 2)
                    if not it.l0:
                        norm(u, 3)

            iterations(act, body)

        @block.vector
        def _(dve):
            nc.vector.memset(eps_c, EPS_ADJ)
            nc.vector.memset(eps1_c, EPS_LN)
            nc.vector.memset(minus_c, -1.0)
            nc.vector.memset(half_c, -0.5).then_inc(s_half, 1)
            dve.wait_ge(s_whi, 1)
            nc.vector.scalar_tensor_tensor(out=flat(w_lo["q"]), in0=flat(xT_land[1]), scalar=-SCALE0,
                                           in1=flat(w_hi["q"]).bitcast(f32), op0=ALU.mult,
                                           op1=ALU.subtract).then_inc(s_wlo, 1)
            dve.wait_ge(s_whi, 2)
            nc.vector.tensor_tensor(flat(w_lo["k"]), flat(v_sb), flat(w_hi["k"]).bitcast(f32),
                                    ALU.subtract).then_inc(s_wlo, 1)

            def x_low_chunk(t, par, c):
                dve.wait_ge(s["act_x"], nth("act_x", t, c))
                nc.vector.tensor_tensor(x_lo[:, c, :], xT_land[par][:, c, :], x_hi[:, c, :].bitcast(f32),
                                        ALU.subtract).then_inc(s["dve_x"], 1)

            for c in range(C):
                x_low_chunk(0, 0, c)
            dve.wait_ge(s_const, 16 * 8)
            nc.vector.tensor_scalar(nbq0_c, bq0_c, -SCALE0, None, ALU.mult)
            nc.vector.tensor_scalar(nbg_c, bg_c, -1.0, None, ALU.mult)
            dve.wait_ge(s_whi, 3)
            for i in range(2):
                half = slice(2 * i, 2 * i + 2)
                op = nc.vector.tensor_tensor(w_lo["v"][:, half, :].rearrange("p a b -> p (a b)"),
                                             flat(probsT[i]),
                                             w_hi["v"][:, half, :].rearrange("p a b -> p (a b)").bitcast(f32),
                                             ALU.subtract)
            op.then_inc(s_wlo, 1)
            for d in range(C):
                dve.wait_ge(s_whi, 4 + d)
                nc.vector.scalar_tensor_tensor(out=w_lo["m"][:, d, :], in0=bank[m_banks[d]][:, :],
                                               scalar=-SCALE1,
                                               in1=w_hi["m"][:, d, :].bitcast(f32), op0=ALU.mult,
                                               op1=ALU.subtract).then_inc(s_wlo, 1)
            dve.wait_ge(s_m, C + 1)
            nc.vector.tensor_scalar(v1_b[:, :], bank[4][:, :], -SCALE1, None, ALU.mult)
            nc.vector.tensor_scalar(r0_c, bank[5][:, 0:1], -SCALE1, None, ALU.mult)
            nc.vector.tensor_scalar(u1_c, bank[5][:, 1:1 + C], -SCALE1, None, ALU.mult).then_inc(s_cst, 1)
            dve.wait_ge(s_cst, 1)
            dve.wait_ge(s_zero, 1)

            def carry_wait(semaphore, value, word):
                dve.wait_ge(semaphore, value)
                nc.vector.memset(carrier[0:1, word:word + 1], 0.0)

            def k_low(t, c):
                dve.wait_ge(s["act_k"], nth("act_k", t, c))
                for e in range(2):
                    r = slice(e * HD, (e + 1) * HD)
                    op = nc.vector.scalar_tensor_tensor(
                        out=k_lo[r, :, e * P:(e + 1) * P],
                        in0=bank[1][r, :].rearrange("p (g j) -> p g j", g=GG), scalar=bk0_c[r, c:c + 1],
                        in1=k_hi[r, :, e * P:(e + 1) * P].bitcast(f32), op0=ALU.add, op1=ALU.subtract)
                op.then_inc(s["dve_k"], 1)

            def q_low(t, c):
                dve.wait_ge(s["act_q"], nth("act_q", t, c))
                nc.vector.scalar_tensor_tensor(out=q_lo[:, :], in0=bank[0][:, :], scalar=nbq0_c[:, c:c + 1],
                                               in1=q_hi[:, :].bitcast(f32), op0=ALU.add,
                                               op1=ALU.subtract).then_inc(s["dve_q"], 1)

            def v_out(t, g):
                dve.wait_ge(s["pe_v"], nth("pe_v", t, g))
                nc.vector.tensor_tensor(v_sb[:, g, :], bank[2 + g % 2][:, :], bv_b[:, :], ALU.add)\
                  .then_inc(s["dve_v"], 1)

            def bias(t):
                dve.wait_ge(s["pe_cb"], nth("pe_cb", t))
                dve.wait_ge(s["act_ln"], nth("act_ln", t))
                for g in range(GG):
                    op = nc.vector.scalar_tensor_tensor(out=bias0[:, g, :], in0=bank[5][:, g * P:(g + 1) * P],
                                                        scalar=a_c[:, g:g + 1], in1=ln_adj[:, g, :],
                                                        op0=ALU.add, op1=ALU.subtract)
                op.then_inc(s["dve_b"], 1)

            def maxima(t, c):
                for h in range(2):
                    if c == 0 and h == 0:
                        dve.wait_ge(s["dve_b"], nth("dve_b", t))
                    carry_wait(s["pe_s"], nth("pe_s", t, 2 * c + h), 2 * c + h)
                    for k in range(h * HALF, (h + 1) * HALF):
                        op = nc.vector.tensor_tensor_reduce(
                            out=probs[:, k, :], in0=bank[4 + h][:, (k % HALF) * P:(k % HALF + 1) * P],
                            in1=bias0[:, k // 2, :], scale=1.0, scalar=BIG, op0=ALU.add, op1=ALU.min,
                            accum_out=nmax[:, k:k + 1])
                    op.then_inc(s["dve_max"], 1)

            def recips(t, c):
                for h in range(2):
                    dve.wait_ge(s["act_exp"], nth("act_exp", t, 2 * c + h))
                    half = slice(h * HALF, (h + 1) * HALF)
                    nc.vector.reciprocal(rcp[:, half], sums[:, half]).then_inc(s["dve_rcp"], 1)

            def residual0(t, c, b, par):
                dve.wait_ge(s["pe_pv"], nth("pe_pv", t, c))
                nc.vector.tensor_tensor(x1T[:, c, :], bank[b][:, :], xT_land[par][:, c, :], ALU.add)\
                  .then_inc(s["dve_pv"], 1)

            def x1lo(t, c):
                dve.wait_ge(s["act_x1"], nth("act_x1", t, c))
                nc.vector.tensor_tensor(x1_lo[:, c, :], x1T[:, c, :], x1_hi[:, c, :].bitcast(f32),
                                        ALU.subtract).then_inc(s["dve_x1"], 1)

            def gates(t, graphs):
                for g in graphs:
                    dve.wait_ge(s_xn[g % 2], 16 * (2 * t + 1 + g // 2))
                    if g > 0:
                        dve.wait_ge(s["dve_a"], nth("dve_a", t, g - 1))
                    nc.vector.tensor_tensor_reduce(out=scratch[:, :], in0=xn[g % 2][:, :], in1=wg1_b[:, :],
                                                   scale=-1.0, scalar=nbg_c, op0=ALU.mult, op1=ALU.add,
                                                   accum_out=a_c[:, g:g + 1])
                    nc.vector.tensor_tensor_reduce(out=xn[g % 2][:, :], in0=xn[g % 2][:, :], in1=wg2_b[:, :],
                                                   scale=-1.0, scalar=0.0, op0=ALU.mult, op1=ALU.add,
                                                   accum_out=c_c[:, g:g + 1]).then_inc(s["dve_a"], 1)

            gates(0, range(GG))

            def body(it):
                t, u = it.t, it.u

                def row_terms(g):
                    dve.wait_ge(s["act_x1n"], nth("act_x1n", u, g))
                    if g > 0:
                        dve.wait_ge(s["dve_r"], nth("dve_r", u, g - 1))
                    elif it.nxt:
                        dve.wait_ge(s["dve_a"], nth("dve_a", t + 1, 1))
                    else:
                        dve.wait_ge(s["dve_a"], nth("dve_a", NG - 1, 3))
                    nc.vector.tensor_tensor_reduce(out=scratch[:, :], in0=x1n[:, g, :], in1=v1_b[:, :],
                                                   scale=1.0, scalar=r0_c, op0=ALU.mult, op1=ALU.add,
                                                   accum_out=r_c[:, g:g + 1]).then_inc(s["dve_r"], 1)

                def masked_scores():
                    par_u = 1 - it.par
                    dve.wait_ge(s["dve_r"], nth("dve_r", u, 3))
                    nc.vector.tensor_scalar(flat(mask), flat(adj_sb[par_u]), 0.0, None, ALU.not_equal)
                    nc.vector.tensor_scalar(scratch[:, :], flat(adj_sb[par_u]), 0.0, MASKED, ALU.is_equal,
                                            ALU.mult).then_inc(s["dve_mask"], 1)
                    dve.wait_ge(s["dve_mask"], nth("dve_mask", u))
                    dve.wait_ge(s["pe_sa"], nth("pe_sa", u))
                    for g in range(GG):
                        op = nc.vector.scalar_tensor_tensor(out=att1[:, g, :],
                                                            in0=bank[0][:, g * P:(g + 1) * P],
                                                            scalar=r_c[:, g:g + 1], in1=mask[:, g, :],
                                                            op0=ALU.add, op1=ALU.mult)
                    op.then_inc(s["dve_sa"], 1)
                    dve.wait_ge(s["dve_sa"], nth("dve_sa", u))
                    nc.vector.tensor_tensor(flat(att1), flat(att1), scratch[:, :], ALU.add)\
                      .then_inc(s["dve_sub"], 1)
                    dve.wait_ge(s["dve_sub"], nth("dve_sub", u))
                    nc.vector.tensor_reduce(nmax1, att1[:, :, :], AX.X, ALU.min).then_inc(s["dve_max1"], 1)

                def attention1():
                    dve.wait_ge(s["act_exp1"], nth("act_exp1", u))
                    nc.vector.reciprocal(rcp1, sums1).then_inc(s["dve_rcp1"], 1)
                    dve.wait_ge(s["dve_rcp1"], nth("dve_rcp1", u))
                    for g in range(GG):
                        op = nc.vector.scalar_tensor_tensor(out=att1[:, g, :], in0=att1[:, g, :],
                                                            scalar=rcp1[:, g:g + 1], in1=mask[:, g, :],
                                                            op0=ALU.mult, op1=ALU.mult)
                    op.then_inc(s["dve_att1"], 1)

                def att1T_low():
                    dve.wait_ge(s["act_tp"], nth("act_tp", u))
                    nc.vector.tensor_tensor(flat(att1T_lo), bank[5][:, :], flat(att1T_hi).bitcast(f32),
                                            ALU.subtract).then_inc(s["dve_tp"], 1)

                def y_low(g):
                    dve.wait_ge(s["act_y"], nth("act_y", u, g))
                    nc.vector.tensor_tensor(y_lo[g % 2][:, :], bank[y_bank(g)][:, :],
                                            y_hi[g % 2][:, :].bitcast(f32), ALU.subtract)\
                      .then_inc(s["dve_y"], 1)

                def residual1(g, b):
                    dve.wait_ge(s["pe_ctx"], nth("pe_ctx", u, g))
                    nc.vector.tensor_tensor(x1n[:, g, :], bank[b][:, :], x1n[:, g, :], ALU.add)\
                      .then_inc(s["dve_res"], 1)
                    dve.wait_ge(s["dve_res"], nth("dve_res", u, g))
                    nc.vector.bn_stats(bnst[:, :], x1n[:, g, :]).then_inc(s["dve_bn"], 1)
                    carry_wait(s["dve_bn"], nth("dve_bn", u, g), 2 * C + g)
                    nc.vector.bn_aggr(lnst[:, g, 0:2], bnst[:, :]).then_inc(s["dve_mean"], 1)

                if it.l0:
                    bias(t)
                    k_low(t, 0)
                    q_low(t, 0)
                    if it.l1:
                        dve.wait_ge(s["pe_pv"], nth("pe_pv", u, 3))
                    v_out(t, 0)
                if it.l1:
                    residual0(u, 3, 6, 1 - it.par)
                if it.l0:
                    v_out(t, 1)
                if it.l1:
                    x1lo(u, 3)
                if it.l0:
                    maxima(t, 0)
                    v_out(t, 2)
                    v_out(t, 3)
                    recips(t, 0)
                    k_low(t, 1)
                    q_low(t, 1)
                if it.nxt:
                    dve.wait_ge(s["dve_a"], nth("dve_a", t, 3))
                    gates(t + 1, (0, 1))
                if it.l1:
                    for g in range(GG):
                        row_terms(g)
                if it.l0:
                    maxima(t, 1)
                if it.l1:
                    masked_scores()
                if it.l0:
                    recips(t, 1)
                if it.l1:
                    attention1()
                    y_low(0)
                    y_low(1)
                if it.l0:
                    k_low(t, 2)
                if it.l1:
                    att1T_low()
                if it.l0:
                    q_low(t, 2)
                if it.nxt:
                    gates(t + 1, (2,))
                if it.l1:
                    residual1(0, 2)
                    residual1(1, 3)
                    y_low(2)
                if it.nxt:
                    gates(t + 1, (3,))
                if it.l1:
                    y_low(3)
                if not it.l1:
                    dve.wait_ge(s_whi, 8)
                    nc.vector.tensor_tensor(flat(w_lo["c"]), flat(x1T), flat(w_hi["c"]).bitcast(f32),
                                            ALU.subtract).then_inc(s_wlo, 1)
                    dve.wait_ge(s_wlo, 8)
                if it.l0:
                    residual0(t, 0, 6, it.par)
                    maxima(t, 2)
                    residual0(t, 1, 7, it.par)
                    x1lo(t, 0)
                    x1lo(t, 1)
                    recips(t, 2)
                    k_low(t, 3)
                    q_low(t, 3)
                if it.nxt:
                    for c in range(C):
                        x_low_chunk(t + 1, 1 - it.par, c)
                if it.l0:
                    maxima(t, 3)
                    residual0(t, 2, 6, it.par)
                if it.l1:
                    residual1(2, 2)
                if it.l0:
                    recips(t, 3)
                if it.l1:
                    residual1(3, 3)
                if it.l0:
                    x1lo(t, 2)

            iterations(dve, body)

        @block.gpsimd
        def _(pool):
            nc.gpsimd.memset(k_hi[:, :, :].bitcast(f32), 0.0)
            nc.gpsimd.memset(k_lo[:, :, :].bitcast(f32), 0.0).then_inc(s_zero, 1)

            pool.wait_ge(s_half, 1)

            def probabilities(t, c):
                for h in range(2):
                    half = slice(h * HALF, (h + 1) * HALF)
                    pool.wait_ge(s["dve_rcp"], nth("dve_rcp", t, 2 * c + h))
                    nc.gpsimd.tensor_tensor(probs[:, half, :], probs[:, half, :],
                                            rcp[:, half].unsqueeze(2).to_broadcast([P, HALF, P]), ALU.mult)\
                        .then_inc(s["pool_p"], 1)

            def body(it):
                t, u = it.t, it.u

                def sigma(g):
                    pool.wait_ge(s["dve_mean"], nth("dve_mean", u, g))
                    nc.gpsimd.tensor_tensor(lnst[:, g, 0:1], lnst[:, g, 0:1], minus_c, ALU.mult)
                    nc.gpsimd.tensor_tensor(lnst[:, g, 3:4], lnst[:, g, 1:2], eps1_c, ALU.add)\
                        .then_inc(s["pool_eps"], 1)
                    pool.wait_ge(s["pool_eps"], nth("pool_eps", u, g))
                    nc.gpsimd.tensor_tensor(lnst[:, g, 2:3], lnst[:, g, 3:4], half_c, ALU.pow)\
                        .then_inc(s["pool_rstd"], 1)
                    pool.wait_ge(s["pool_rstd"], nth("pool_rstd", u, g))
                    nc.gpsimd.tensor_tensor(lnst[:, g, 3:4], lnst[:, g, 0:1], lnst[:, g, 2:3], ALU.mult)\
                        .then_inc(s["pool_nmr"], 1)

                def affine(g):
                    pool.wait_ge(s["act_nrm"], nth("act_nrm", u, g))
                    nc.gpsimd.tensor_tensor(x1n[:, g, :], x1n[:, g, :], gamma_b[:, :], ALU.mult)\
                        .then_inc(s["pool_gam"], 1)
                    pool.wait_ge(s["pool_gam"], nth("pool_gam", u, g))
                    nc.gpsimd.tensor_tensor(x1n[:, g, :], x1n[:, g, :], beta_b[:, :], ALU.add)\
                        .then_inc(s["pool_out"], 1)

                if it.l0:
                    probabilities(t, 0)
                    probabilities(t, 1)
                if it.l1:
                    for g in range(2):
                        sigma(g)
                    for g in range(2):
                        affine(g)
                if it.l0:
                    probabilities(t, 2)
                if it.l1:
                    sigma(2)
                if it.l0:
                    probabilities(t, 3)
                if it.l1:
                    sigma(3)
                    for g in range(2, 4):
                        affine(g)

            iterations(pool, body)



def kernel(x, adj, L0_gnn_W_q, L0_gnn_b_q, L0_gnn_W_k, L0_gnn_b_k, L0_gnn_W_v, L0_gnn_b_v, L0_gnn_w_g,
           L0_gnn_b_g, L1_gnn_Wq, L1_gnn_bq, L1_gnn_Wk, L1_gnn_bk, L1_gnn_Wc, L1_gnn_gamma,
           L1_gnn_beta):
    import numpy as np
    import concourse.bacc as bacc
    from concourse import mybir as mb
    from concourse.bass_utils import run_bass_kernel_spmd

    def host(a):
        return np.asarray(a)

    def chunks(w):
        return host(w).reshape(C, P, -1).transpose(1, 0, 2)

    xs = host(x)
    arrays = {
        "xT": xs.reshape(NG, COLS, C, P).transpose(0, 3, 2, 1).reshape(NG * P, C * COLS),
        "x": xs.reshape(GRAPHS * P, D),
        "adj": host(adj),
        "wq": chunks(L0_gnn_W_q), "wk": chunks(L0_gnn_W_k), "wv": chunks(L0_gnn_W_v),
        "wqT1": chunks(host(L1_gnn_Wq).T), "wkT1": chunks(host(L1_gnn_Wk).T), "wc": chunks(L1_gnn_Wc),
        "bq0": host(L0_gnn_b_q).reshape(C, P).T, "bk0": host(L0_gnn_b_k).reshape(C, P).T,
        "bv0": host(L0_gnn_b_v).reshape(1, D), "wg": host(L0_gnn_w_g).reshape(1, 2 * D),
        "bg": host(L0_gnn_b_g).reshape(1, 1),
        "bq1": host(L1_gnn_bq).reshape(C, P).T, "bk1": host(L1_gnn_bk).reshape(C, P).T,
        "gamma": host(L1_gnn_gamma).reshape(1, D), "beta": host(L1_gnn_beta).reshape(1, D),
        "ident_in": np.eye(P, dtype=np.float32),
    }
    arrays = {n: np.ascontiguousarray(a) for n, a in arrays.items()}
    nc = bacc.Bacc("TRN2", target_bir_lowering=False, num_devices=1, dynamic_dma_scratch_size=1024)
    ins = {n: nc.dram_tensor(f"in_{n}", a.shape, mb.dt.from_np(a.dtype), kind="ExternalInput").ap()
           for n, a in arrays.items()}
    out = nc.dram_tensor("out", (GRAPHS * P, D), mb.dt.float32, kind="ExternalOutput").ap()
    gnn_program(nc, out=out, **ins)
    r = run_bass_kernel_spmd(nc, [{f"in_{n}": a for n, a in arrays.items()}], core_ids=[0])
    return r.results[0]["out"].reshape(GRAPHS, P, D)
```

```python
from collections import namedtuple
from contextlib import ExitStack

import concourse.bass as bass
from concourse import mybir

P = 128
GRAPHS = 128
D = 512
HEADS = 8
HD = D // HEADS
C = D // P
GG = 4
NG = GRAPHS // GG
COLS = GG * P
PAIR = 2 * GG
HALF = PAIR // 2
EPS_ADJ = 1e-9
EPS_LN = 1e-5
MASKED = 1e18
SCALE0 = float(HD) ** -0.5
SCALE1 = float(D) ** -0.5
BIG = 3.0e38


Iteration = namedtuple("Iteration", "t u p par l0 l1 second nxt")


def gnn_program(nc, xT, x, adj, wq, wk, wv, wqT1, wkT1, wc, bq0, bk0, bv0, wg, bg, bq1, bk1,
                gamma, beta, ident_in, out):
    f32 = mybir.dt.float32
    f32r = mybir.dt.float32r
    bf16 = mybir.dt.bfloat16
    ALU = mybir.AluOpType
    ACT = mybir.ActivationFunctionType
    AX = mybir.AxisListType

    adj_v = adj.rearrange("g i j -> i g j")

    with ExitStack() as ctx:
        def sb(name, shape, dt=f32):
            return ctx.enter_context(nc.sbuf_tensor(name, shape, dt))

        def sem(name):
            return ctx.enter_context(nc.semaphore(name))

        def flat(t):
            return t[:, :, :].rearrange("p a b -> p (a b)")

        w_hi = {n: sb(f"w{n}_hi", [P, C, D], f32r) for n in "qkvmc"}
        w_lo = {n: sb(f"w{n}_lo", [P, C, D], f32r) for n in "qkvmc"}
        xT_land = [sb(f"xT_land{i}", [P, C, COLS]) for i in range(2)]
        x_hi = sb("x_hi", [P, C, COLS], f32r)
        x_lo = sb("x_lo", [P, C, COLS], f32r)
        q_hi = sb("q_hi", [P, COLS], f32r)
        q_lo = sb("q_lo", [P, COLS], f32r)
        k_hi = sb("k_hi", [P, GG, 2 * P], f32r)
        k_lo = sb("k_lo", [P, GG, 2 * P], f32r)
        v_sb = sb("v_sb", [P, GG, D])
        probs = sb("probs", [P, PAIR, P])
        probsT = [sb(f"probsT{i}", [P, PAIR, P]) for i in range(2)]
        x1T = sb("x1T", [P, C, COLS])
        x1_hi = sb("x1_hi", [P, C, COLS], f32r)
        x1_lo = sb("x1_lo", [P, C, COLS], f32r)
        g_sb = [sb(f"g_sb{i}", [P, COLS]) for i in range(2)]
        y_hi = [sb(f"y_hi{i}", [P, D], f32r) for i in range(2)]
        y_lo = [sb(f"y_lo{i}", [P, D], f32r) for i in range(2)]
        x1n = sb("x1n", [P, GG, D])
        xn = [sb(f"xn{i}", [P, D]) for i in range(2)]
        xn_first = [xn[0][:, :], xn[1][:, :], flat(probs)[:, 0:D], flat(probs)[:, D:2 * D]]
        adj_sb = [sb(f"adj_sb{i}", [P, GG, P]) for i in range(2)]
        ln_adj = sb("ln_adj", [P, GG, P])
        bias0 = sb("bias0", [P, GG, P])
        mask = sb("mask", [P, GG, P], bf16)
        att1 = sb("att1", [P, GG, P])
        att1T_hi = sb("att1T_hi", [P, GG, P], f32r)
        att1T_lo = sb("att1T_lo", [P, GG, P], f32r)
        scratch = sb("scratch", [P, D])
        bv_b = sb("bv_b", [P, D])
        gamma_b = sb("gamma_b", [P, D])
        beta_b = sb("beta_b", [P, D])
        wq1_land = [g_sb[0][:, :], g_sb[1][:, :], flat(att1), beta_b[:, :]]
        wg1_b = sb("wg1_b", [P, D])
        wg2_b = sb("wg2_b", [P, D])
        v1_b = sb("v1_b", [P, D])
        ident = sb("ident", [P, P])
        cols = sb("cols", [P, 4 * C])
        bq0_c, bk0_c, bq1_c, bk1_c = (cols[:, C * i:C * (i + 1)] for i in range(4))
        consts = sb("consts", [P, 16])
        bg_c, nbg_c, r0_c, half_c, eps_c, eps1_c, minus_c = (consts[:, i:i + 1] for i in range(7))
        u1_c = consts[:, 8:8 + C]
        nbq0_c = consts[:, 12:12 + C]
        carrier = sb("carrier", [P, 2 * C + GG])
        a_c = sb("a_c", [P, GG])
        c_c = sb("c_c", [P, GG])
        r_c = sb("r_c", [P, GG])
        nmax = sb("nmax", [P, PAIR])
        sums = sb("sums", [P, PAIR])
        rcp = sb("rcp", [P, PAIR])
        stats1 = sb("stats1", [P, 3 * GG])
        nmax1, sums1, rcp1 = (stats1[:, GG * i:GG * (i + 1)] for i in range(3))
        bnst = sb("bnst", [P, 6])
        lnst = sb("lnst", [P, GG, 4])

        bank = [ctx.enter_context(nc.psum_tensor(f"bank{i}", [P, 512], f32)) for i in range(8)]

        PER = dict(pe_q=4, pe_k=4, pe_cb=1, pe_s=8, pe_t=8, pe_v=4, pe_pv=4, pe_g=4, pe_x=4, pe_sa=1,
                   pe_y=4, pe_tp=1, pe_ctx=4,
                   act_q=4, act_k=4, act_exp=2 * C, act_pt=2 * C, act_x1=4, act_g=4, act_x1n=4,
                   act_y=4, act_ln=1, act_exp1=1, act_tp=1, act_nrm=4,
                   dve_q=4, dve_k=4, dve_b=1, dve_max=2 * C, dve_rcp=2 * C, dve_v=4, dve_pv=4,
                   dve_x1=4, dve_a=4, dve_r=4, dve_mask=1, dve_sa=1, dve_sub=1, dve_max1=1,
                   dve_rcp1=1, dve_att1=1, dve_tp=1, dve_y=4, dve_res=4, dve_bn=4, dve_mean=4,
                   dve_x=4, act_x=4, pool_p=2 * C, pool_eps=4, pool_rstd=4, pool_nmr=4,
                   pool_gam=4, pool_out=4)
        s = {n: sem(n) for n in PER}
        s_xT = [sem(f"xT_loaded{i}") for i in range(2)]
        s_adj = [sem(f"adj_loaded{i}") for i in range(2)]
        s_xn = [sem(f"xn_loaded{i}") for i in range(2)]
        s_out = [sem(f"out_stored{i}") for i in range(GG)]
        s_wld = {n: [sem(f"w{n}_chunk{d}_loaded") for d in range(C)] for n in "qkv"}
        s_x0 = [sem(f"x0_chunk{d}_loaded") for d in range(C)]
        s_wld1 = {n: sem(f"w{n}_loaded") for n in ("q1", "k1", "c")}
        s_cols = sem("cols_loaded")
        s_const = sem("const_loaded")
        s_rows = sem("rows_loaded")
        s_beta = sem("beta_loaded")
        s_zero = sem("pool_zeroed")
        s_hi = {n: sem(f"act_w{n}_hi") for n in "qkvmc"}
        s_lo = {n: sem(f"dve_w{n}_lo") for n in "qkvmc"}
        s_m = sem("pe_m")
        m_banks = (6, 7, 2, 3)
        s_const1 = sem("const1_loaded")
        s_cst = sem("dve_const")
        s_cst1 = sem("dve_const1")
        s_half = sem("dve_half")
        s_last = sem("dve_last_out")

        def nth(name, t, k=0):
            return t * PER[name] + k + 1

        def g_bank(c, last):
            return bank[(2, 3, 0, 1)[c] if last else 2 + c % 2]

        def x_bank(g, last):
            return bank[(7, 5)[g % 2] if last else 1]

        def sa_bank(last):
            return bank[6 if last else 0]

        def y_bank(g, last):
            return bank[((4, 2, 3, 0) if last else (2, 3, 0, 1))[g]]

        def y_split(g, last):
            return (x_hi[:, g, :], x_lo[:, g, :]) if last else (y_hi[g % 2][:, :], y_lo[g % 2][:, :])

        def tp_bank(last):
            return bank[1 if last else 5]

        def ctx_bank(g, last):
            return bank[(7, 5, 6, 4)[g] if last else 2 + g % 2]

        def hi_lo(out_ap, st, mv):
            for i in range(len(st)):
                last = hi_lo_part(out_ap, st[i], mv[i], i == 0, i == len(st) - 1)
            return last

        def hi_lo_part(out_ap, st, mv, start, stop):
            nc.tensor.matmul(out_ap, st[0], mv[0], start=start, stop=False)
            nc.tensor.matmul(out_ap, st[0], mv[1], start=False, stop=False)
            return nc.tensor.matmul(out_ap, st[1], mv[0], start=False, stop=stop)

        def w_cols(n, c):
            return [(w_hi[n][:, d, c * P:(c + 1) * P], w_lo[n][:, d, c * P:(c + 1) * P]) for d in range(C)]

        def w_rows(n):
            return [(w_hi[n][:, d, :], w_lo[n][:, d, :]) for d in range(C)]

        def act_cols(hi, lo):
            return [(hi[:, d, :], lo[:, d, :]) for d in range(C)]

        def act_rows(hi, lo, g):
            return [(hi[:, d, g * P:(g + 1) * P], lo[:, d, g * P:(g + 1) * P]) for d in range(C)]

        def iterations(eng, body):
            def step(p, par, **kinds):
                t = 2 * p + par
                body(Iteration(**{**dict(t=t, u=t - 1, p=p, par=par, l0=True, l1=True, second=False,
                                         nxt=True), **kinds}))
            step(0, 0, l1=False)
            step(0, 1, second=True)
            with eng.Fori(1, NG // 2 - 1) as p:
                step(p, 0)
                step(p, 1)
            step(NG // 2 - 1, 0)
            step(NG // 2 - 1, 1, nxt=False)
            step(NG // 2, 0, l0=False, nxt=False)

        block = ctx.enter_context(nc.Block())

        @block.sync
        def _(sp):
            def load_xT(t, par):
                sp.dma_start(flat(xT_land[par]), xT[bass.ds(t * P, P), :]).then_inc(s_xT[par], 16)

            def load_adj(t, par):
                sp.dma_start(adj_sb[par][:, :, :], adj_v[:, bass.ds(t * GG, GG), :]).then_inc(s_adj[par], 16)

            def load_xn(t, g):
                sp.dma_start(xn[g % 2][:, :], x[bass.ds(t * COLS + g * P, P), :]).then_inc(s_xn[g % 2], 16)

            for d in range(C):
                sp.dma_start(v_sb[:, d, :], wk[:, d, :]).then_inc(s_wld["k"][d], 16)
                sp.dma_start(xT_land[0][:, d, :], xT[0:P, d * COLS:(d + 1) * COLS]).then_inc(s_x0[d], 16)
            for d in range(C):
                sp.dma_start(xT_land[1][:, d, :], wq[:, d, :]).then_inc(s_wld["q"][d], 16)
            sp.dma_start(bq0_c, bq0).then_inc(s_cols, 16)
            sp.dma_start(bk0_c, bk0).then_inc(s_cols, 16)
            sp.dma_start(bg_c, bg.to_broadcast([P, 1])).then_inc(s_cols, 16)
            for d in range(C):
                sp.dma_start(probsT[d // 2][:, (d % 2) * HALF:(d % 2 + 1) * HALF, :]
                             .rearrange("p a b -> p (a b)"), wv[:, d, :]).then_inc(s_wld["v"][d], 16)
            sp.dma_start(wg1_b[:, :], wg[:, 0:D].to_broadcast([P, D])).then_inc(s_const, 16)
            sp.dma_start(wg2_b[:, :], wg[:, D:2 * D].to_broadcast([P, D])).then_inc(s_const, 16)
            for g in range(GG):
                sp.dma_start(xn_first[g], x[g * P:(g + 1) * P, :]).then_inc(s_xn[g % 2], 16)
            sp.dma_start(ident[:, :], ident_in).then_inc(s_const, 16)
            load_adj(0, 0)
            for d in range(C):
                sp.dma_start(wq1_land[d], wqT1[:, d, :]).then_inc(s_wld1["q1"], 16)
            sp.dma_start(x1n[:, :, :], wkT1).then_inc(s_wld1["k1"], 16)
            sp.dma_start(bv_b[:, :], bv0.to_broadcast([P, D])).then_inc(s_rows, 16)
            sp.dma_start(gamma_b[:, :], gamma.to_broadcast([P, D])).then_inc(s_rows, 16)
            sp.dma_start(bq1_c, bq1).then_inc(s_const1, 16)
            sp.dma_start(bk1_c, bk1).then_inc(s_const1, 16)
            sp.dma_start(x1T[:, :, :], wc).then_inc(s_wld1["c"], 16)

            def body(it):
                t, u = it.t, it.u
                if it.nxt:
                    if it.l1:
                        sp.wait_ge(s["dve_pv"], nth("dve_pv", u, 3))
                    else:
                        sp.wait_ge(s_lo["q"], C)
                    load_xT(t + 1, 1 - it.par)
                    for g in range(2):
                        sp.wait_ge(s["dve_a"], nth("dve_a", t, g + 2))
                        load_xn(t + 1, g)
                    if it.l1:
                        sp.wait_ge(s["dve_mask"], nth("dve_mask", u))
                    load_adj(t + 1, 1 - it.par)

                def store(g):
                    if it.l0 or g == 0:
                        sp.wait_ge(s["pool_out"], nth("pool_out", u, g))
                    else:
                        sp.wait_ge(s_last, 2 * g)
                    sp.dma_start(out[bass.ds(u * COLS + g * P, P), :], x1n[:, g, :]).then_inc(s_out[g], 16)

                if it.nxt:
                    for g in range(2, 4):
                        sp.wait_ge(s["dve_a"], nth("dve_a", t + 1, g - 2))
                        load_xn(t + 1, g)
                if it.l1:
                    for g in range(GG) if it.l0 else (1, 2, 0, 3):
                        store(g)
                else:
                    sp.wait_ge(s_m, C + 1)
                    sp.dma_start(beta_b[:, :], beta.to_broadcast([P, D])).then_inc(s_beta, 16)

            iterations(sp, body)
            for g in range(GG):
                sp.wait_ge(s_out[g], 16 * NG)

        @block.tensor
        def _(pe):
            def m_chunk(d):
                if d == 0:
                    pe.wait_ge(s_wld1["q1"], 16 * C)
                    pe.wait_ge(s_wld1["k1"], 16)
                for f in range(C):
                    mm = nc.tensor.matmul(bank[m_banks[d]][:, :],
                                          wq1_land[f][:, d * P:(d + 1) * P], x1n[:, f, :],
                                          start=(f == 0), stop=(f == C - 1))
                mm.then_inc(s_m, 1)

            def m_row_term():
                pe.wait_ge(s_const1, 16 * 2)
                pe.wait_ge(s_lo["m"], 3)
                for f in range(C):
                    mm = nc.tensor.matmul(bank[2][:, :], bk1_c[:, f:f + 1].to_broadcast([P, P]),
                                          wq1_land[f], start=(f == 0), stop=(f == C - 1))
                mm.then_inc(s_m, 1)

            def m_columns():
                pe.wait_ge(s_lo["m"], 4)
                for f in range(C):
                    nc.tensor.matmul(bank[3][:, 0:1], bk1_c[:, f:f + 1].to_broadcast([P, P]),
                                     bq1_c[:, f:f + 1], start=(f == 0), stop=(f == C - 1))
                for d in range(C):
                    for f in range(C):
                        mm = nc.tensor.matmul(bank[3][:, 1 + d:2 + d], x1n[:, f, d * P:(d + 1) * P],
                                              bq1_c[:, f:f + 1], start=(f == 0), stop=(f == C - 1))
                mm.then_inc(s_m, 1)

            def project_k(t, c):
                for d in range(C):
                    if c == 0:
                        pe.wait_ge(s["dve_x"], nth("dve_x", t, d))
                    mm = hi_lo_part(bank[1][:, :], w_cols("k", c)[d], act_cols(x_hi, x_lo)[d], d == 0, d == C - 1)
                mm.then_inc(s["pe_k"], 1)

            def project_q(t, c, first=False):
                for d in range(C):
                    if first:
                        pe.wait_ge(s_lo["q"], d + 1)
                    mm = hi_lo_part(bank[0][:, :], w_cols("q", c)[d], act_cols(x_hi, x_lo)[d], d == 0, d == C - 1)
                mm.then_inc(s["pe_q"], 1)

            def v(t, g, first, second):
                if g < 2 and not first and not second:
                    pe.wait_ge(s["dve_res"], nth("dve_res", t - 2, g + 2))
                if g < 2 and second:
                    pe.wait_ge(s_cst1, 2)
                if g >= 2:
                    pe.wait_ge(s["dve_v"], nth("dve_v", t, g - 2))
                hi_lo(bank[2 + g % 2][:, :], act_rows(x_hi, x_lo, g), w_rows("v")).then_inc(s["pe_v"], 1)

            def scores(t, c):
                pe.wait_ge(s["dve_q"], nth("dve_q", t, c))
                pe.wait_ge(s["dve_k"], nth("dve_k", t, c))
                for g in range(GG):
                    if g == 0 and c > 0:
                        pe.wait_ge(s["dve_max"], nth("dve_max", t, 2 * c - 2))
                    if g == 2 and c > 0:
                        pe.wait_ge(s["dve_max"], nth("dve_max", t, 2 * c - 1))
                    if g == 2 and c == 0:
                        pe.wait_ge(s["dve_b"], nth("dve_b", t))
                    cols_g = slice(g * P, (g + 1) * P)
                    mm = hi_lo(bank[4 + g // 2][:, (g % 2) * 2 * P:(g % 2 + 1) * 2 * P],
                               [(q_hi[:, cols_g], q_lo[:, cols_g])], [(k_hi[:, g, :], k_lo[:, g, :])])
                    if g % 2:
                        mm.then_inc(s["pe_s"], 1)

            def turn(t, c):
                for h in range(2):
                    pe.wait_ge(s["pool_p"], nth("pool_p", t, 2 * c + h))
                    for k in range(HALF):
                        mm = nc.tensor.transpose(bank[6 + h][:, k * P:(k + 1) * P],
                                                 probs[:, h * HALF + k, :], ident[:, :])
                    mm.then_inc(s["pe_t"], 1)

            def pv(t, c, b):
                for h in range(2):
                    pe.wait_ge(s["act_pt"], nth("act_pt", t, 2 * c + h))
                    if c == 0 and h == 0:
                        pe.wait_ge(s["dve_v"], nth("dve_v", t, GG - 1))
                    for g in range(2 * h, 2 * h + 2):
                        for e in range(2):
                            mm = nc.tensor.matmul(bank[b][e * HD:(e + 1) * HD, g * P:(g + 1) * P],
                                                  v_sb[:, g, c * P + e * HD:c * P + (e + 1) * HD],
                                                  probsT[c % 2][:, 2 * g + e, :], start=True, stop=True)
                mm.then_inc(s["pe_pv"], 1)

            def layer1_alone(u):
                def part(out_bank, st, mv, d):
                    return hi_lo_part(out_bank[:, :], st[d], mv[d], d == 0, d == C - 1)

                def g_part(c, d):
                    return part(g_bank(c, True), w_cols("m", c), act_cols(x1_hi, x1_lo), d)

                def y_part(g, d):
                    return part(y_bank(g, True), act_rows(x1_hi, x1_lo, g), w_rows("c"), d)

                def xw(g):
                    for d in range(C):
                        mm = nc.tensor.transpose(x_bank(g, True)[:, d * P:(d + 1) * P],
                                                 x1T[:, d, g * P:(g + 1) * P], ident[:, :])
                    mm.then_inc(s["pe_x"], 1)

                def sa(c):
                    pe.wait_ge(s["act_g"], nth("act_g", u, c))
                    for g in range(GG):
                        cols_g = slice(g * P, (g + 1) * P)
                        mm = nc.tensor.matmul(sa_bank(True)[:, cols_g], g_sb[c % 2][:, cols_g],
                                              x1T[:, c, cols_g], start=(c == 0 and g == 0),
                                              stop=(c == C - 1), skip_group_check=True)
                    if c == C - 1:
                        mm.then_inc(s["pe_sa"], 1)

                pe.wait_ge(s["dve_x1"], nth("dve_x1", u, 1))
                for c in range(C):
                    if c < 2:
                        pe.wait_ge(s["dve_res"], nth("dve_res", u - 1, c + 2))
                    elif c == 2:
                        pe.wait_ge(s["dve_q"], nth("dve_q", u, C - 1))
                    else:
                        pe.wait_ge(s["dve_k"], nth("dve_k", u, C - 1))
                    g_part(c, 0)
                    g_part(c, 1)
                pe.wait_ge(s["dve_x1"], nth("dve_x1", u, 2))
                for c in range(C):
                    g_part(c, 2)
                pe.wait_ge(s["dve_pv"], nth("dve_pv", u, 2))
                pe.wait_ge(s["act_pt"], nth("act_pt", u, 5))
                turn(u, 3)
                pv(u, 3, 6)
                pe.wait_ge(s["dve_max"], nth("dve_max", u, 2 * C - 1))
                for d in range(C - 1):
                    y_part(0, d)
                pe.wait_ge(s["dve_x1"], nth("dve_x1", u, 3))
                for c in range(C):
                    g_part(c, C - 1).then_inc(s["pe_g"], 1)
                pe.wait_ge(s["act_pt"], nth("act_pt", u, 7))
                xw(0)
                xw(1)
                sa(0)
                pe.wait_ge(s["act_x1n"], nth("act_x1n", u, 0))
                xw(2)
                sa(1)
                pe.wait_ge(s["act_x1n"], nth("act_x1n", u, 1))
                xw(3)
                sa(2)
                sa(3)
                y_part(0, C - 1).then_inc(s["pe_y"], 1)
                for y in range(1, GG):
                    pe.wait_ge(s["act_g"], nth("act_g", u, y - 1))
                    if y == GG - 1:
                        pe.wait_ge(s["act_g"], nth("act_g", u, C - 1))
                        pe.wait_ge(s["dve_att1"], nth("dve_att1", u))
                        for g in range(GG):
                            mm = nc.tensor.transpose(tp_bank(True)[:, g * P:(g + 1) * P], att1[:, g, :],
                                                     ident[:, :])
                        mm.then_inc(s["pe_tp"], 1)
                    for d in range(C):
                        mm = y_part(y, d)
                    mm.then_inc(s["pe_y"], 1)
                pe.wait_ge(s["dve_tp"], nth("dve_tp", u))
                pe.wait_ge(s["act_x1n"], nth("act_x1n", u, 3))
                for g in range(GG):
                    pe.wait_ge(s["dve_y"], nth("dve_y", u, g))
                    hi_lo(ctx_bank(g, True)[:, :], [(att1T_hi[:, g, :], att1T_lo[:, g, :])],
                          [y_split(g, True)]).then_inc(s["pe_ctx"], 1)

            def body(it):
                t, u = it.t, it.u
                first, second = not it.l1, it.second
                if not it.l0:
                    return layer1_alone(u)
                if not first:
                    pe.wait_ge(s["dve_k"], nth("dve_k", t - 1, 3))
                project_k(t, 0)
                if not first:
                    pe.wait_ge(s["dve_q"], nth("dve_q", t - 1, 3))
                project_q(t, 0, first)
                if first:
                    pe.wait_ge(s_lo["v"], C)
                    v(t, 0, first, second)
                    v(t, 1, first, second)
                    m_chunk(0)
                else:
                    pe.wait_ge(s["dve_max"], nth("dve_max", t - 1, 2 * C - 1))
                pe.wait_ge(s["dve_a"], nth("dve_a", t, 3))
                for g in range(GG):
                    mm = nc.tensor.transpose(bank[5][:, g * P:(g + 1) * P],
                                             c_c[:, g:g + 1].to_broadcast([P, P]), ident[:, :])
                mm.then_inc(s["pe_cb"], 1)
                if first:
                    m_chunk(1)
                else:
                    v(t, 0, first, second)
                    pe.wait_ge(s["dve_pv"], nth("dve_pv", u, 2))
                    pe.wait_ge(s["act_pt"], nth("act_pt", u, 5))
                    turn(u, 3)
                    v(t, 1, first, second)
                    pv(u, 3, 6)
                scores(t, 0)
                v(t, 2, first, second)
                v(t, 3, first, second)
                project_k(t, 1)
                project_q(t, 1)

                def gw(c):
                    if c < 2:
                        pe.wait_ge(s["dve_v"], nth("dve_v", t, c + 2))
                        if c == 0:
                            pe.wait_ge(s["dve_x1"], nth("dve_x1", u, 3))
                    else:
                        pe.wait_ge(s["act_g"], nth("act_g", u, c - 2))
                    hi_lo(g_bank(c, False)[:, :], w_cols("m", c), act_cols(x1_hi, x1_lo)).then_inc(s["pe_g"], 1)

                def xw(g):
                    if g == 0:
                        pe.wait_ge(s["dve_k"], nth("dve_k", t, 1))
                    else:
                        pe.wait_ge(s["act_x1n"], nth("act_x1n", u, g - 1))
                    for d in range(C):
                        mm = nc.tensor.transpose(bank[1][:, d * P:(d + 1) * P],
                                                 x1T[:, d, g * P:(g + 1) * P], ident[:, :])
                    mm.then_inc(s["pe_x"], 1)

                def sa(c):
                    if c == 0:
                        pe.wait_ge(s["dve_q"], nth("dve_q", t, 1))
                    pe.wait_ge(s["act_g"], nth("act_g", u, c))
                    for g in range(GG):
                        cols_g = slice(g * P, (g + 1) * P)
                        mm = nc.tensor.matmul(bank[0][:, cols_g], g_sb[c % 2][:, cols_g], x1T[:, c, cols_g],
                                              start=(c == 0 and g == 0), stop=(c == C - 1),
                                              skip_group_check=True)
                    if c == C - 1:
                        mm.then_inc(s["pe_sa"], 1)

                def yw(g):
                    if g < 2:
                        pe.wait_ge(s["act_g"], nth("act_g", u, g + 2))
                    hi_lo(y_bank(g, False)[:, :], act_rows(x1_hi, x1_lo, g), w_rows("c")).then_inc(s["pe_y"], 1)

                def cx(g):
                    pe.wait_ge(s["dve_y"], nth("dve_y", u, g))
                    hi_lo(ctx_bank(g, False)[:, :], [(att1T_hi[:, g, :], att1T_lo[:, g, :])],
                          [y_split(g, False)]).then_inc(s["pe_ctx"], 1)

                if not first:
                    gw(0)
                    xw(0)
                    gw(1)
                    xw(1)
                    pe.wait_ge(s["dve_pv"], nth("dve_pv", u, 3))
                    pe.wait_ge(s["act_pt"], nth("act_pt", u, 7))
                else:
                    pe.wait_ge(s_lo["m"], 2)
                turn(t, 0)
                if not first:
                    sa(0)
                    gw(2)
                    xw(2)
                    sa(1)
                    gw(3)
                    xw(3)
                    sa(2)
                scores(t, 1)
                if not first:
                    sa(3)
                    yw(0)
                    yw(1)
                    pe.wait_ge(s["act_x1n"], nth("act_x1n", u, 3))
                project_k(t, 2)
                if not first:
                    pe.wait_ge(s["dve_sa"], nth("dve_sa", u))
                    pe.wait_ge(s["dve_max"], nth("dve_max", t, 3))
                    pe.wait_ge(s["dve_att1"], nth("dve_att1", u))
                    for g in range(GG):
                        mm = nc.tensor.transpose(bank[5][:, g * P:(g + 1) * P], att1[:, g, :], ident[:, :])
                    mm.then_inc(s["pe_tp"], 1)
                project_q(t, 2)
                if first:
                    pe.wait_ge(s["dve_v"], nth("dve_v", t, 3))
                    m_chunk(2)
                pe.wait_ge(s["act_pt"], nth("act_pt", t, 1))
                turn(t, 1)
                if not first:
                    pe.wait_ge(s["dve_tp"], nth("dve_tp", u))
                    cx(0)
                    cx(1)
                    pe.wait_ge(s["dve_q"], nth("dve_q", t, 2))
                    yw(2)
                    pe.wait_ge(s["dve_k"], nth("dve_k", t, 2))
                    yw(3)
                pe.wait_ge(s["act_pt"], nth("act_pt", t, 2))
                pv(t, 0, 6)
                if not first:
                    pe.wait_ge(s["dve_tp"], nth("dve_tp", u))
                scores(t, 2)
                pe.wait_ge(s["act_pt"], nth("act_pt", t, 3))
                pv(t, 1, 7)
                if not first:
                    pe.wait_ge(s["dve_y"], nth("dve_y", u, 3))
                project_k(t, 3)
                project_q(t, 3)
                if first:
                    m_chunk(3)
                    m_row_term()
                if not first:
                    pe.wait_ge(s["dve_res"], nth("dve_res", u, 1))
                    cx(2)
                pe.wait_ge(s["dve_pv"], nth("dve_pv", t, 0))
                pe.wait_ge(s["dve_pv"], nth("dve_pv", t, 1))
                turn(t, 2)
                if not first:
                    cx(3)
                scores(t, 3)
                if first:
                    m_columns()
                pv(t, 2, 6)

            iterations(pe, body)

        @block.scalar
        def _(act):
            def x_hi_chunk(par, c):
                nc.scalar.activation(x_hi[:, c, :], xT_land[par][:, c, :], ACT.Copy).then_inc(s["act_x"], 1)

            def m_high(d):
                act.wait_ge(s_m, d + 1)
                nc.scalar.activation(w_hi["m"][:, d, :], bank[m_banks[d]][:, :], ACT.Copy, scale=-SCALE1)\
                  .then_inc(s_hi["m"], 1)

            for d in range(C):
                act.wait_ge(s_wld["k"][d], 16)
                nc.scalar.activation(w_hi["k"][:, d, :], v_sb[:, d, :], ACT.Copy).then_inc(s_hi["k"], 1)
                act.wait_ge(s_x0[d], 16)
                x_hi_chunk(0, d)
            for d in range(C):
                act.wait_ge(s_wld["q"][d], 16)
                nc.scalar.activation(w_hi["q"][:, d, :], xT_land[1][:, d, :], ACT.Copy, scale=-SCALE0)\
                  .then_inc(s_hi["q"], 1)
            for d in range(C):
                act.wait_ge(s_wld["v"][d], 16)
                nc.scalar.activation(w_hi["v"][:, d, :],
                                     probsT[d // 2][:, (d % 2) * HALF:(d % 2 + 1) * HALF, :]
                                     .rearrange("p a b -> p (a b)"), ACT.Copy).then_inc(s_hi["v"], 1)
            act.wait_ge(s_cst, 1)
            act.wait_ge(s_zero, 1)

            def log_adj(t, loads, par):
                act.wait_ge(s_adj[par], 16 * loads)
                nc.scalar.activation(ln_adj[:, :, :], adj_sb[par][:, :, :], ACT.Ln,
                                     bias=eps_c).then_inc(s["act_ln"], 1)

            log_adj(0, 1, 0)

            def k_high(t, c):
                act.wait_ge(s["pe_k"], nth("pe_k", t, c))
                for e in range(2):
                    r = slice(e * HD, (e + 1) * HD)
                    op = nc.scalar.activation(k_hi[r, :, e * P:(e + 1) * P],
                                              bank[1][r, :].rearrange("p (g j) -> p g j", g=GG),
                                              ACT.Identity, bias=bk0_c[r, c:c + 1])
                op.then_inc(s["act_k"], 1)

            def q_high(t, c):
                act.wait_ge(s["pe_q"], nth("pe_q", t, c))
                nc.scalar.activation(q_hi[:, :], bank[0][:, :], ACT.Identity,
                                     bias=nbq0_c[:, c:c + 1]).then_inc(s["act_q"], 1)

            def exps(t, c):
                for h in range(2):
                    act.wait_ge(s["dve_max"], nth("dve_max", t, 2 * c + h))
                    for k in range(h * HALF, (h + 1) * HALF):
                        op = nc.scalar.activation(probs[:, k, :], probs[:, k, :], ACT.Exp,
                                                  bias=nmax[:, k:k + 1], scale=-1.0,
                                                  accum_out=sums[:, k:k + 1])
                    op.then_inc(s["act_exp"], 1)

            def turned(t, c):
                for h in range(2):
                    act.wait_ge(s["pe_t"], nth("pe_t", t, 2 * c + h))
                    nc.scalar.activation(probsT[c % 2][:, h * HALF:(h + 1) * HALF, :]
                                         .rearrange("p a b -> p (a b)"),
                                         bank[6 + h][:, :], ACT.Copy).then_inc(s["act_pt"], 1)

            def x1hi(t, c):
                act.wait_ge(s["dve_pv"], nth("dve_pv", t, c))
                nc.scalar.activation(x1_hi[:, c, :], x1T[:, c, :], ACT.Copy).then_inc(s["act_x1"], 1)

            def body(it):
                t, u, last = it.t, it.u, not it.l0

                def g_out(c):
                    if it.second and c == 0:
                        act.wait_ge(s_cst1, 2)
                    act.wait_ge(s["pe_g"], nth("pe_g", u, c))
                    if last and c >= 2:
                        act.wait_ge(s["pe_x"], nth("pe_x", u, c))
                    nc.scalar.activation(g_sb[c % 2][:, :], g_bank(c, last)[:, :], ACT.Identity,
                                         bias=u1_c[:, c:c + 1]).then_inc(s["act_g"], 1)

                def x1_out(g):
                    act.wait_ge(s["pe_x"], nth("pe_x", u, g))
                    if not it.second:
                        act.wait_ge(s_out[g], 16 * u)
                    nc.scalar.activation(x1n[:, g, :], x_bank(g, last)[:, :], ACT.Copy).then_inc(s["act_x1n"], 1)

                def y_out(g):
                    act.wait_ge(s["pe_y"], nth("pe_y", u, g))
                    nc.scalar.activation(y_split(g, last)[0], y_bank(g, last)[:, :], ACT.Copy)\
                      .then_inc(s["act_y"], 1)

                def norm(u, g):
                    act.wait_ge(s["pool_nmr"], nth("pool_nmr", u, g))
                    nc.scalar.activation(x1n[:, g, :], x1n[:, g, :], ACT.Identity,
                                         bias=lnst[:, g, 3:4], scale=lnst[:, g, 2:3]).then_inc(s["act_nrm"], 1)

                if it.l0:
                    k_high(t, 0)
                    q_high(t, 0)
                if it.l1:
                    turned(u, 3)
                    if not it.second:
                        norm(u - 1, 3)
                    x1hi(u, 3)
                if it.l0:
                    if not it.l1:
                        m_high(0)
                        m_high(1)
                    exps(t, 0)
                    k_high(t, 1)
                    q_high(t, 1)
                if it.l1:
                    g_out(0)
                    x1_out(0)
                    g_out(1)
                    x1_out(1)
                if it.l0:
                    turned(t, 0)
                if it.l1:
                    if last:
                        x1_out(2)
                        g_out(2)
                        x1_out(3)
                        g_out(3)
                    else:
                        g_out(2)
                        x1_out(2)
                        g_out(3)
                        x1_out(3)
                if it.l0:
                    exps(t, 1)
                if it.l1:
                    act.wait_ge(s["dve_max1"], nth("dve_max1", u))
                    for g in range(GG):
                        op = nc.scalar.activation(att1[:, g, :], att1[:, g, :], ACT.Exp,
                                                  bias=nmax1[:, g:g + 1], scale=-1.0,
                                                  accum_out=sums1[:, g:g + 1])
                    op.then_inc(s["act_exp1"], 1)
                    y_out(0)
                    y_out(1)
                    if last:
                        y_out(2)
                if it.l0:
                    k_high(t, 2)
                if it.l1:
                    act.wait_ge(s["pe_tp"], nth("pe_tp", u))
                    nc.scalar.activation(flat(att1T_hi), tp_bank(last)[:, :], ACT.Copy).then_inc(s["act_tp"], 1)
                if it.l0:
                    q_high(t, 2)
                    if not it.l1:
                        m_high(2)
                    turned(t, 1)
                if it.l1:
                    if not last:
                        y_out(2)
                        norm(u, 0)
                    y_out(3)
                    if last:
                        norm(u, 0)
                    norm(u, 1)
                if not it.l1:
                    act.wait_ge(s_wld1["c"], 16)
                    nc.scalar.activation(w_hi["c"][:, :, :], x1T[:, :, :], ACT.Copy).then_inc(s_hi["c"], 1)
                if it.l0:
                    x1hi(t, 0)
                    exps(t, 2)
                    x1hi(t, 1)
                    k_high(t, 3)
                    q_high(t, 3)
                    if not it.l1:
                        m_high(3)
                if it.nxt:
                    act.wait_ge(s["pe_q"], nth("pe_q", t, C - 1))
                    act.wait_ge(s_xT[1 - it.par], 16 * (it.p + 1))
                    x_hi_chunk(1 - it.par, 0)
                    x_hi_chunk(1 - it.par, 1)
                if it.l0:
                    turned(t, 2)
                if it.nxt:
                    x_hi_chunk(1 - it.par, 2)
                    x_hi_chunk(1 - it.par, 3)
                if it.l0:
                    exps(t, 3)
                    x1hi(t, 2)
                if it.nxt:
                    act.wait_ge(s["dve_b"], nth("dve_b", t))
                    log_adj(t + 1, it.p + 1 + it.par, 1 - it.par)
                if it.l1:
                    norm(u, 2)
                    if not it.l0:
                        norm(u, 3)

            iterations(act, body)

        @block.vector
        def _(dve):
            nc.vector.memset(eps_c, EPS_ADJ)
            nc.vector.memset(eps1_c, EPS_LN)
            nc.vector.memset(minus_c, -1.0)
            nc.vector.memset(half_c, -0.5).then_inc(s_half, 1)
            def x_low_chunk(t, par, c):
                dve.wait_ge(s["act_x"], nth("act_x", t, c))
                nc.vector.tensor_tensor(x_lo[:, c, :], xT_land[par][:, c, :], x_hi[:, c, :].bitcast(f32),
                                        ALU.subtract).then_inc(s["dve_x"], 1)

            def m_low(d):
                dve.wait_ge(s_hi["m"], d + 1)
                nc.vector.scalar_tensor_tensor(out=w_lo["m"][:, d, :], in0=bank[m_banks[d]][:, :],
                                               scalar=-SCALE1,
                                               in1=w_hi["m"][:, d, :].bitcast(f32), op0=ALU.mult,
                                               op1=ALU.subtract).then_inc(s_lo["m"], 1)

            for d in range(C):
                dve.wait_ge(s_hi["k"], d + 1)
                nc.vector.tensor_tensor(w_lo["k"][:, d, :], v_sb[:, d, :], w_hi["k"][:, d, :].bitcast(f32),
                                        ALU.subtract).then_inc(s_lo["k"], 1)
                x_low_chunk(0, 0, d)
            for d in range(C):
                dve.wait_ge(s_hi["q"], d + 1)
                nc.vector.scalar_tensor_tensor(out=w_lo["q"][:, d, :], in0=xT_land[1][:, d, :],
                                               scalar=-SCALE0, in1=w_hi["q"][:, d, :].bitcast(f32),
                                               op0=ALU.mult, op1=ALU.subtract).then_inc(s_lo["q"], 1)
            dve.wait_ge(s_cols, 16 * 3)
            nc.vector.tensor_scalar(nbq0_c, bq0_c, -SCALE0, None, ALU.mult)
            nc.vector.tensor_scalar(nbg_c, bg_c, -1.0, None, ALU.mult).then_inc(s_cst, 1)
            for d in range(C):
                dve.wait_ge(s_hi["v"], d + 1)
                nc.vector.tensor_tensor(w_lo["v"][:, d, :],
                                        probsT[d // 2][:, (d % 2) * HALF:(d % 2 + 1) * HALF, :]
                                        .rearrange("p a b -> p (a b)"), w_hi["v"][:, d, :].bitcast(f32),
                                        ALU.subtract).then_inc(s_lo["v"], 1)
            dve.wait_ge(s_cst, 1)
            dve.wait_ge(s_zero, 1)

            def carry_wait(semaphore, value, word):
                dve.wait_ge(semaphore, value)
                nc.vector.memset(carrier[0:1, word:word + 1], 0.0)

            def k_low(t, c):
                dve.wait_ge(s["act_k"], nth("act_k", t, c))
                for e in range(2):
                    r = slice(e * HD, (e + 1) * HD)
                    op = nc.vector.scalar_tensor_tensor(
                        out=k_lo[r, :, e * P:(e + 1) * P],
                        in0=bank[1][r, :].rearrange("p (g j) -> p g j", g=GG), scalar=bk0_c[r, c:c + 1],
                        in1=k_hi[r, :, e * P:(e + 1) * P].bitcast(f32), op0=ALU.add, op1=ALU.subtract)
                op.then_inc(s["dve_k"], 1)

            def q_low(t, c):
                dve.wait_ge(s["act_q"], nth("act_q", t, c))
                nc.vector.scalar_tensor_tensor(out=q_lo[:, :], in0=bank[0][:, :], scalar=nbq0_c[:, c:c + 1],
                                               in1=q_hi[:, :].bitcast(f32), op0=ALU.add,
                                               op1=ALU.subtract).then_inc(s["dve_q"], 1)

            def v_out(t, g):
                dve.wait_ge(s["pe_v"], nth("pe_v", t, g))
                nc.vector.tensor_tensor(v_sb[:, g, :], bank[2 + g % 2][:, :], bv_b[:, :], ALU.add)\
                  .then_inc(s["dve_v"], 1)

            def bias(t):
                dve.wait_ge(s["pe_cb"], nth("pe_cb", t))
                dve.wait_ge(s["act_ln"], nth("act_ln", t))
                for g in range(GG):
                    op = nc.vector.scalar_tensor_tensor(out=bias0[:, g, :], in0=bank[5][:, g * P:(g + 1) * P],
                                                        scalar=a_c[:, g:g + 1], in1=ln_adj[:, g, :],
                                                        op0=ALU.add, op1=ALU.subtract)
                op.then_inc(s["dve_b"], 1)

            def maxima(t, c):
                for h in range(2):
                    if c == 0 and h == 0:
                        dve.wait_ge(s["dve_b"], nth("dve_b", t))
                    carry_wait(s["pe_s"], nth("pe_s", t, 2 * c + h), 2 * c + h)
                    for k in range(h * HALF, (h + 1) * HALF):
                        op = nc.vector.tensor_tensor_reduce(
                            out=probs[:, k, :], in0=bank[4 + h][:, (k % HALF) * P:(k % HALF + 1) * P],
                            in1=bias0[:, k // 2, :], scale=1.0, scalar=BIG, op0=ALU.add, op1=ALU.min,
                            accum_out=nmax[:, k:k + 1])
                    op.then_inc(s["dve_max"], 1)

            def recips(t, c):
                for h in range(2):
                    dve.wait_ge(s["act_exp"], nth("act_exp", t, 2 * c + h))
                    half = slice(h * HALF, (h + 1) * HALF)
                    nc.vector.reciprocal(rcp[:, half], sums[:, half]).then_inc(s["dve_rcp"], 1)

            def residual0(t, c, b, par):
                dve.wait_ge(s["pe_pv"], nth("pe_pv", t, c))
                nc.vector.tensor_tensor(x1T[:, c, :], bank[b][:, :], xT_land[par][:, c, :], ALU.add)\
                  .then_inc(s["dve_pv"], 1)

            def x1lo(t, c):
                dve.wait_ge(s["act_x1"], nth("act_x1", t, c))
                nc.vector.tensor_tensor(x1_lo[:, c, :], x1T[:, c, :], x1_hi[:, c, :].bitcast(f32),
                                        ALU.subtract).then_inc(s["dve_x1"], 1)

            def gates(t, graphs):
                for g in graphs:
                    dve.wait_ge(s_xn[g % 2], 16 * (2 * t + 1 + g // 2))
                    gate(xn[g % 2][:, :], t, g)

            def gate(rows, t, g):
                if g > 0:
                    dve.wait_ge(s["dve_a"], nth("dve_a", t, g - 1))
                nc.vector.tensor_tensor_reduce(out=scratch[:, :], in0=rows, in1=wg1_b[:, :],
                                               scale=-1.0, scalar=nbg_c, op0=ALU.mult, op1=ALU.add,
                                               accum_out=a_c[:, g:g + 1])
                nc.vector.tensor_tensor_reduce(out=rows, in0=rows, in1=wg2_b[:, :],
                                               scale=-1.0, scalar=0.0, op0=ALU.mult, op1=ALU.add,
                                               accum_out=c_c[:, g:g + 1]).then_inc(s["dve_a"], 1)

            dve.wait_ge(s_const, 16 * 3)
            for i in range(2):
                dve.wait_ge(s_xn[i], 16 * 2)
            for g in range(GG):
                gate(xn_first[g], 0, g)
            dve.wait_ge(s_rows, 16 * 2)

            def body(it):
                t, u, last = it.t, it.u, not it.l0

                def row_terms(g):
                    dve.wait_ge(s["act_x1n"], nth("act_x1n", u, g))
                    if g > 0:
                        dve.wait_ge(s["dve_r"], nth("dve_r", u, g - 1))
                    elif it.nxt:
                        dve.wait_ge(s["dve_a"], nth("dve_a", t + 1, 1))
                    else:
                        dve.wait_ge(s["dve_a"], nth("dve_a", NG - 1, 3))
                    nc.vector.tensor_tensor_reduce(out=scratch[:, :], in0=x1n[:, g, :], in1=v1_b[:, :],
                                                   scale=1.0, scalar=r0_c, op0=ALU.mult, op1=ALU.add,
                                                   accum_out=r_c[:, g:g + 1]).then_inc(s["dve_r"], 1)

                def masked_scores():
                    par_u = 1 - it.par
                    dve.wait_ge(s["dve_r"], nth("dve_r", u, 3))
                    nc.vector.tensor_scalar(flat(mask), flat(adj_sb[par_u]), 0.0, None, ALU.not_equal)
                    nc.vector.tensor_scalar(scratch[:, :], flat(adj_sb[par_u]), 0.0, MASKED, ALU.is_equal,
                                            ALU.mult).then_inc(s["dve_mask"], 1)
                    dve.wait_ge(s["dve_mask"], nth("dve_mask", u))
                    dve.wait_ge(s["pe_sa"], nth("pe_sa", u))
                    for g in range(GG):
                        op = nc.vector.scalar_tensor_tensor(out=att1[:, g, :],
                                                            in0=sa_bank(last)[:, g * P:(g + 1) * P],
                                                            scalar=r_c[:, g:g + 1], in1=mask[:, g, :],
                                                            op0=ALU.add, op1=ALU.mult)
                    op.then_inc(s["dve_sa"], 1)
                    dve.wait_ge(s["dve_sa"], nth("dve_sa", u))
                    nc.vector.tensor_tensor(flat(att1), flat(att1), scratch[:, :], ALU.add)\
                      .then_inc(s["dve_sub"], 1)
                    dve.wait_ge(s["dve_sub"], nth("dve_sub", u))
                    nc.vector.tensor_reduce(nmax1, att1[:, :, :], AX.X, ALU.min).then_inc(s["dve_max1"], 1)

                def attention1():
                    dve.wait_ge(s["act_exp1"], nth("act_exp1", u))
                    nc.vector.reciprocal(rcp1, sums1).then_inc(s["dve_rcp1"], 1)
                    dve.wait_ge(s["dve_rcp1"], nth("dve_rcp1", u))
                    for g in range(GG):
                        op = nc.vector.scalar_tensor_tensor(out=att1[:, g, :], in0=att1[:, g, :],
                                                            scalar=rcp1[:, g:g + 1], in1=mask[:, g, :],
                                                            op0=ALU.mult, op1=ALU.mult)
                    op.then_inc(s["dve_att1"], 1)

                def att1T_low():
                    dve.wait_ge(s["act_tp"], nth("act_tp", u))
                    nc.vector.tensor_tensor(flat(att1T_lo), tp_bank(last)[:, :], flat(att1T_hi).bitcast(f32),
                                            ALU.subtract).then_inc(s["dve_tp"], 1)

                def y_low(g):
                    dve.wait_ge(s["act_y"], nth("act_y", u, g))
                    hi, lo = y_split(g, last)
                    nc.vector.tensor_tensor(lo, y_bank(g, last)[:, :], hi.bitcast(f32), ALU.subtract)\
                      .then_inc(s["dve_y"], 1)

                def residual1(g):
                    dve.wait_ge(s["pe_ctx"], nth("pe_ctx", u, g))
                    nc.vector.tensor_tensor(x1n[:, g, :], ctx_bank(g, last)[:, :], x1n[:, g, :], ALU.add)\
                      .then_inc(s["dve_res"], 1)
                    dve.wait_ge(s["dve_res"], nth("dve_res", u, g))
                    nc.vector.bn_stats(bnst[:, :], x1n[:, g, :]).then_inc(s["dve_bn"], 1)
                    carry_wait(s["dve_bn"], nth("dve_bn", u, g), 2 * C + g)
                    nc.vector.bn_aggr(lnst[:, g, 0:2], bnst[:, :]).then_inc(s["dve_mean"], 1)

                if it.l0:
                    bias(t)
                    k_low(t, 0)
                    q_low(t, 0)
                    if it.l1:
                        dve.wait_ge(s["pe_pv"], nth("pe_pv", u, 3))
                    v_out(t, 0)
                if it.l1:
                    residual0(u, 3, 6, 1 - it.par)
                if it.l0:
                    v_out(t, 1)
                if it.l1:
                    x1lo(u, 3)
                if it.l0:
                    maxima(t, 0)
                    if not it.l1:
                        m_low(0)
                        m_low(1)
                    v_out(t, 2)
                    v_out(t, 3)
                    recips(t, 0)
                    k_low(t, 1)
                    q_low(t, 1)
                if it.nxt:
                    dve.wait_ge(s["dve_a"], nth("dve_a", t, 3))
                    gates(t + 1, (0, 1))
                if it.l1:
                    for g in range(GG):
                        row_terms(g)
                if it.l0:
                    maxima(t, 1)
                if it.l1:
                    masked_scores()
                if it.l0:
                    recips(t, 1)
                if it.l1:
                    attention1()
                    y_low(0)
                    y_low(1)
                if it.l0:
                    k_low(t, 2)
                if it.l1:
                    att1T_low()
                if it.l0:
                    q_low(t, 2)
                    if not it.l1:
                        m_low(2)
                if it.nxt:
                    gates(t + 1, (2,))
                if it.l1:
                    if last:
                        y_low(2)
                        y_low(3)
                    residual1(0)
                    residual1(1)
                    if not last:
                        y_low(2)
                if it.nxt:
                    gates(t + 1, (3,))
                if it.l1 and not last:
                    y_low(3)
                if not it.l1:
                    dve.wait_ge(s_hi["c"], 1)
                    nc.vector.tensor_tensor(flat(w_lo["c"]), flat(x1T), flat(w_hi["c"]).bitcast(f32),
                                            ALU.subtract).then_inc(s_lo["c"], 1)
                    dve.wait_ge(s_lo["c"], 1)
                if it.l0:
                    residual0(t, 0, 6, it.par)
                    maxima(t, 2)
                    residual0(t, 1, 7, it.par)
                    x1lo(t, 0)
                    x1lo(t, 1)
                    recips(t, 2)
                    k_low(t, 3)
                    q_low(t, 3)
                if not it.l1:
                    m_low(3)
                    dve.wait_ge(s_m, C + 1)
                    nc.vector.tensor_scalar(v1_b[:, :], bank[2][:, :], -SCALE1, None, ALU.mult)\
                      .then_inc(s_cst1, 1)
                if it.nxt:
                    for c in range(C):
                        x_low_chunk(t + 1, 1 - it.par, c)
                if it.l0:
                    maxima(t, 3)
                if not it.l1:
                    dve.wait_ge(s_m, C + 2)
                    nc.vector.tensor_scalar(r0_c, bank[3][:, 0:1], -SCALE1, None, ALU.mult)
                    nc.vector.tensor_scalar(u1_c, bank[3][:, 1:1 + C], -SCALE1, None, ALU.mult)\
                      .then_inc(s_cst1, 1)
                    dve.wait_ge(s_cst1, 2)
                if it.l0:
                    residual0(t, 2, 6, it.par)
                if it.l1:
                    residual1(2)
                if it.l0:
                    recips(t, 3)
                if it.l1:
                    residual1(3)
                if last:
                    for g in range(1, GG):
                        dve.wait_ge(s["act_nrm"], nth("act_nrm", u, g))
                        nc.vector.tensor_tensor(x1n[:, g, :], x1n[:, g, :], gamma_b[:, :], ALU.mult)\
                          .then_inc(s_last, 1)
                        dve.wait_ge(s_last, 2 * g - 1)
                        nc.vector.tensor_tensor(x1n[:, g, :], x1n[:, g, :], beta_b[:, :], ALU.add)\
                          .then_inc(s_last, 1)
                if it.l0:
                    x1lo(t, 2)

            iterations(dve, body)

        @block.gpsimd
        def _(pool):
            nc.gpsimd.memset(k_hi[:, :, :].bitcast(f32), 0.0)
            nc.gpsimd.memset(k_lo[:, :, :].bitcast(f32), 0.0).then_inc(s_zero, 1)

            pool.wait_ge(s_half, 1)
            pool.wait_ge(s_rows, 16 * 2)

            def probabilities(t, c):
                for h in range(2):
                    half = slice(h * HALF, (h + 1) * HALF)
                    pool.wait_ge(s["dve_rcp"], nth("dve_rcp", t, 2 * c + h))
                    nc.gpsimd.tensor_tensor(probs[:, half, :], probs[:, half, :],
                                            rcp[:, half].unsqueeze(2).to_broadcast([P, HALF, P]), ALU.mult)\
                        .then_inc(s["pool_p"], 1)

            def body(it):
                t, u = it.t, it.u

                def sigma(g):
                    pool.wait_ge(s["dve_mean"], nth("dve_mean", u, g))
                    nc.gpsimd.tensor_tensor(lnst[:, g, 0:1], lnst[:, g, 0:1], minus_c, ALU.mult)
                    nc.gpsimd.tensor_tensor(lnst[:, g, 3:4], lnst[:, g, 1:2], eps1_c, ALU.add)\
                        .then_inc(s["pool_eps"], 1)
                    pool.wait_ge(s["pool_eps"], nth("pool_eps", u, g))
                    nc.gpsimd.tensor_tensor(lnst[:, g, 2:3], lnst[:, g, 3:4], half_c, ALU.pow)\
                        .then_inc(s["pool_rstd"], 1)
                    pool.wait_ge(s["pool_rstd"], nth("pool_rstd", u, g))
                    nc.gpsimd.tensor_tensor(lnst[:, g, 3:4], lnst[:, g, 0:1], lnst[:, g, 2:3], ALU.mult)\
                        .then_inc(s["pool_nmr"], 1)

                def affine(g):
                    pool.wait_ge(s["act_nrm"], nth("act_nrm", u, g))
                    nc.gpsimd.tensor_tensor(x1n[:, g, :], x1n[:, g, :], gamma_b[:, :], ALU.mult)\
                        .then_inc(s["pool_gam"], 1)
                    if it.second and g == 0:
                        pool.wait_ge(s_beta, 16)
                    pool.wait_ge(s["pool_gam"], nth("pool_gam", u, g))
                    nc.gpsimd.tensor_tensor(x1n[:, g, :], x1n[:, g, :], beta_b[:, :], ALU.add)\
                        .then_inc(s["pool_out"], 1)

                if it.l0:
                    probabilities(t, 0)
                    probabilities(t, 1)
                if not it.l0:
                    for g in range(GG):
                        sigma(g)
                    affine(0)
                    return
                if it.l1:
                    for g in range(2):
                        sigma(g)
                    for g in range(2):
                        affine(g)
                if it.l0:
                    probabilities(t, 2)
                if it.l1:
                    sigma(2)
                if it.l0:
                    probabilities(t, 3)
                if it.l1:
                    sigma(3)
                    for g in range(2, 4):
                        affine(g)

            iterations(pool, body)


def kernel(x, adj, L0_gnn_W_q, L0_gnn_b_q, L0_gnn_W_k, L0_gnn_b_k, L0_gnn_W_v, L0_gnn_b_v, L0_gnn_w_g,
           L0_gnn_b_g, L1_gnn_Wq, L1_gnn_bq, L1_gnn_Wk, L1_gnn_bk, L1_gnn_Wc, L1_gnn_gamma,
           L1_gnn_beta):
    import numpy as np
    import concourse.bacc as bacc
    from concourse import mybir as mb
    from concourse.bass_utils import run_bass_kernel_spmd

    def host(a):
        return np.asarray(a)

    def chunks(w):
        return host(w).reshape(C, P, -1).transpose(1, 0, 2)

    xs = host(x)
    arrays = {
        "xT": xs.reshape(NG, COLS, C, P).transpose(0, 3, 2, 1).reshape(NG * P, C * COLS),
        "x": xs.reshape(GRAPHS * P, D),
        "adj": host(adj),
        "wq": chunks(L0_gnn_W_q), "wk": chunks(L0_gnn_W_k), "wv": chunks(L0_gnn_W_v),
        "wqT1": chunks(host(L1_gnn_Wq).T), "wkT1": chunks(host(L1_gnn_Wk).T), "wc": chunks(L1_gnn_Wc),
        "bq0": host(L0_gnn_b_q).reshape(C, P).T, "bk0": host(L0_gnn_b_k).reshape(C, P).T,
        "bv0": host(L0_gnn_b_v).reshape(1, D), "wg": host(L0_gnn_w_g).reshape(1, 2 * D),
        "bg": host(L0_gnn_b_g).reshape(1, 1),
        "bq1": host(L1_gnn_bq).reshape(C, P).T, "bk1": host(L1_gnn_bk).reshape(C, P).T,
        "gamma": host(L1_gnn_gamma).reshape(1, D), "beta": host(L1_gnn_beta).reshape(1, D),
        "ident_in": np.eye(P, dtype=np.float32),
    }
    arrays = {n: np.ascontiguousarray(a) for n, a in arrays.items()}
    nc = bacc.Bacc("TRN2", target_bir_lowering=False, num_devices=1, dynamic_dma_scratch_size=1024)
    ins = {n: nc.dram_tensor(f"in_{n}", a.shape, mb.dt.from_np(a.dtype), kind="ExternalInput").ap()
           for n, a in arrays.items()}
    out = nc.dram_tensor("out", (GRAPHS * P, D), mb.dt.float32, kind="ExternalOutput").ap()
    gnn_program(nc, out=out, **ins)
    r = run_bass_kernel_spmd(nc, [{f"in_{n}": a for n, a in arrays.items()}], core_ids=[0])
    return r.results[0]["out"].reshape(GRAPHS, P, D)
```
